# Optimizing a Trainium2 kernel written in Bass

```python
import numpy as np
import jax
import jax.numpy as jnp

def _softmax(x, axis=-1):
    return jax.nn.softmax(x, axis=axis)
def _gelu(x):
    return jax.nn.gelu(x, approximate=True)
def _silu(x):
    return jax.nn.silu(x)
def _sigmoid(x):
    return jax.nn.sigmoid(x)
def _layernorm(x, axis=-1, eps=1e-5):
    m = jnp.mean(x, axis=axis, keepdims=True)
    v = jnp.var(x, axis=axis, keepdims=True)
    return (x - m) / jnp.sqrt(v + eps)
def _scatter_add(tgt, idx, src, axis=0):
    return tgt.at[idx].add(src)
def _segment_sum(src, seg, n):
    return jax.ops.segment_sum(src, seg, n)

kernel_name = 'mk_adj_preln_d1_adj_256_a331c0'

def setup_inputs(seed: int = 0):
    np.random.seed(seed)
    _w = jnp.asarray
    def _rec_inputs():
        import jax
        import jax.numpy as jnp
        _gk = jax.random.key(seed)
        x = -0.0005146 + 1 * jax.random.normal(jax.random.fold_in(_gk, 1), (8, 2048, 256), jnp.float32)
        _w = (1.0 + jnp.arange(2048, dtype=jnp.float32)) ** -0.5
        _w = _w / _w.mean()
        _pij = jnp.clip(0.00195312 * _w[:, None] * _w[None, :], 0.0, 1.0)
        _a = jax.random.uniform(jax.random.fold_in(_gk, 2), (8, 2048, 2048)) < _pij
        adj = _a.astype(jnp.int32)
        return x, adj
    x, adj = _rec_inputs()
    def _L0_gnn_setup():
        import jax, jax.numpy as jnp
        import numpy as np
        B, N, C, OUT, S = (4, 2048, 256, 256, 25)
        DENSITY = 0.008
        key = jax.random.key(seed)
        kA, kX, kW = jax.random.split(key, 3)
        A = jax.random.bernoulli(kA, DENSITY, (B, N, N)).astype(jnp.int32)
        X = jax.random.normal(kX, (B, N, C), dtype=jnp.float32)
        W = jax.random.normal(kW, (2 * C, OUT), dtype=jnp.float32) * np.float32(1.0 / np.sqrt(2 * C))
        b = jnp.zeros((OUT,), dtype=jnp.float32)
        return {'A': A, 'X': X, 'W': W, 'b': b}
    _L0_gnn_all = _L0_gnn_setup()
    _L0_gnn_in = {k: v for k, v in _L0_gnn_all.items() if k in ('W', 'b', )}
    del _L0_gnn_all

    return {
        "x": x,
        "adj": adj,
        "L0_gnn_W": _L0_gnn_in["W"],
        "L0_gnn_b": _L0_gnn_in["b"],
    }

def reference(x, adj, L0_gnn_W, L0_gnn_b):
    import jax
    import jax.numpy as jnp
    def _L0_gnn_ref(A, X, W, b):
        import jax, jax.numpy as jnp
        import numpy as np
        B, N, C, OUT, S = (4, 2048, 256, 256, 25)
        DENSITY = 0.008
        mask = A != 0
        neg_inf = jnp.float32(-jnp.inf)
        pri = -jnp.arange(N, dtype=jnp.float32)
        scores = jnp.where(mask, pri, neg_inf)
        vals, idx = jax.lax.top_k(scores, S)
        valid = vals > neg_inf
        feats = jax.vmap(lambda x, i: x[i])(X, idx)
        feats = jnp.where(valid[..., None], feats, neg_inf)
        agg = feats.max(axis=2)
        degree = mask.sum(axis=-1)
        agg = jnp.where((degree <= S)[..., None], jnp.maximum(agg, 0.0), agg)
        h = jnp.concatenate([X, agg], axis=-1)
        out = jax.nn.relu(jnp.einsum('bnf,fo->bno', h, W) + b)
        return out

    h = jnp.maximum(_layernorm(x, axis=-1), 0.0)
    x = x + _L0_gnn_ref(adj, h, L0_gnn_W, L0_gnn_b)
    return x


_drawn_inputs = setup_inputs


def setup_inputs(seed=0):
    import zlib

    import numpy as np

    out = dict(_drawn_inputs(seed))
    spreads = {'L0_gnn_b': (0.0, 0.1)}
    factors = {}
    for name, (base, spread) in spreads.items():
        noise = np.random.default_rng([zlib.crc32(name.encode()), seed]).standard_normal(out[name].shape)
        drawn = base * np.exp(spread * noise) if base else spread * noise
        out[name] = jnp.asarray(drawn.astype(out[name].dtype))
    for name, factor in factors.items():
        out[name] = (out[name] * factor).astype(out[name].dtype)
    return out
```

```python
from contextlib import ExitStack

import concourse.bass as bass
from concourse import mybir

ALU = mybir.AluOpType
ACT = mybir.ActivationFunctionType
F32 = mybir.dt.float32
BF16 = mybir.dt.bfloat16
I32 = mybir.dt.int32
U32 = mybir.dt.uint32
I16 = mybir.dt.int16
U16 = mybir.dt.uint16
I8 = mybir.dt.int8
U8 = mybir.dt.uint8
AX_X = mybir.AxisListType.X

P = 128
S = 25
LIGHT = 8
GROUP = 16
QT = 4
RING_A, RING_B = 4, 2
SKIP = 1 << 20
CREDIT = 32
EPS = 1e-5


def value(batch, per_batch, more):
    return batch * per_batch + more


def due(level):
    return not isinstance(level, int) or level > 0


class Steps:

    def __init__(self, base):
        self.base, self.n = base, 0

    def up(self):
        self.n += 1
        return 1

    @property
    def now(self):
        return self.base + self.n


def build(nc, x, adj, w, b, out):
    B, N, C = x.shape
    OUT = w.shape[1]
    NT = N // P
    NQ = NT // QT
    NG = N // GROUP
    WORDS = N // 32
    KC = 2 * C // P
    NV = S + 1
    NSLOT = S - 1
    COLS = 2 * LIGHT + 2
    HG = 32
    assert NT == 16 and NG == P and C == OUT == 256 and KC == 4

    x_rows = x.rearrange("b (t p) c -> b p t c", p=P)
    out_rows = out.rearrange("b (t p) c -> b p t c", p=P)
    adj_rows = adj.rearrange("b (t p) j -> b t p j", p=P)
    h_dram = [nc.dram_tensor(f"h_table{i}", [N, C], F32).ap() for i in range(2)]
    agg_dram = [nc.dram_tensor(f"agg_table{i}", [N, C], F32).ap() for i in range(2)]
    bits_dram = nc.dram_tensor("bits_table", [N, WORDS], U32).ap()
    h_rows = [d.rearrange("(t p) c -> p t c", p=P) for d in h_dram]
    agg_rows = [d.rearrange("(t p) c -> p t c", p=P) for d in agg_dram]
    bits_rows = bits_dram.rearrange("(t p) j -> p t j", p=P)

    with ExitStack() as ctx:
        def sb(name, shape, dt):
            return ctx.enter_context(nc.sbuf_tensor(name, shape, dt))

        def ps(name, shape):
            return ctx.enter_context(nc.psum_tensor(name, shape, F32))

        def sem(name):
            return ctx.enter_context(nc.semaphore(name))

        ident = sb("ident", [P, P], F32)
        before = sb("before", [P, P], BF16)
        ones_bf = sb("ones_bf", [P, P], BF16)
        ones_f = sb("ones_f", [P, NV * NT], F32)
        zeros = sb("zeros", [P, C], F32)
        eps = sb("eps", [P, 1], F32)
        w_sb = sb("w_sb", [P, KC, OUT], F32)
        b_sb = sb("b_sb", [1, OUT], F32)
        position = sb("position", [P, N], I16)
        group_no = sb("group_no", [P, NG], F32)
        group_late = sb("group_late", [P, NG], F32)
        bit_late = sb("bit_late", [P, GROUP], F32)
        bit_of = sb("bit_of", [P, GROUP], I32)
        pick = sb("pick", [P, GROUP], I32)
        counts_down = sb("counts_down", [P, NV], F32)
        iota_i = sb("iota_i", [P, P], I32)
        row_in_tile = sb("row_in_tile", [P, 1], F32)
        tile_no = sb("tile_no", [P, NT], F32)

        xs = sb("xs", [P, 2, NT, C], F32)
        adj_in = sb("adj_in", [P, 4, N], I32)
        signs = sb("signs", [P, 2, QT, N], I8)
        work_a = sb("work_a", [P, QT * N // 8], U32)
        work_b = sb("work_b", [P, QT * N // 8], U32)
        half1 = work_a[:, :]
        half2 = work_b[:, 0:QT * N // 16]
        keys = work_b[:, QT * NG:2 * QT * NG].bitcast(I32).rearrange("p (t g) -> p t g", t=QT)
        cand = work_a[:, 0:QT * 8 * GROUP].bitcast(I32).rearrange("p (t g i) -> p t g i", t=QT, g=8)
        pop_a = work_a[:, :].bitcast(U16)
        pop_b = work_b[:, :].bitcast(U16)
        heavy_bit = work_a[:, 0:HG * GROUP].bitcast(I32).rearrange("p (g i) -> p g i", i=GROUP)
        heavy_pos = work_b[:, 0:HG * GROUP].bitcast(F32).rearrange("p (g i) -> p g i", i=GROUP)
        bits = sb("bits", [P, NT, WORDS], U32)
        top_groups = sb("top_groups", [P, QT, 8], I32)
        found = sb("found", [P, NT, 8], I32)
        found_f = sb("found_f", [P, NT * 8], F32)
        carried = sb("carried", [P, NT, COLS], BF16)
        count = sb("count", [P, NT], F32)
        onehot = sb("onehot", [P, NV, NT], BF16)
        cum = sb("cum", [P, NV * NT], F32)
        spot = sb("spot", [P, NV * NT], F32)
        rank = sb("rank", [P, NT], F32)
        select = sb("select", [P, 2, N], BF16)
        tiles_f = sb("tiles_f", [P, S], I32)
        n_tiles = sb("n_tiles", [P, 2, S], I32)
        ranked = sb("ranked", [P, NT, COLS], F32)
        slot_of = sb("slot_of", [P, NT * 8], F32)
        no_slot = sb("no_slot", [P, NT * 8], F32)
        row_of = sb("row_of", [P, NT], F32)
        perm = sb("perm", [P, 2, NT], U32)
        idx = sb("idx", [P, S, NT], U32)
        stats = sb("stats", [P, NT, 6], F32)
        mean_var = sb("mean_var", [P, NT, 2], F32)
        std = sb("std", [P, NT], F32)
        rstd = sb("rstd", [P, 2, NT], F32)
        shift = sb("shift", [P, 2, NT], F32)
        h_out = sb("h_out", [P, 2, QT, C], F32)
        heavy_bits = sb("heavy_bits", [P, NT, WORDS], U32)
        heavy_key = sb("heavy_key", [P, NG], F32)
        heavy_groups = sb("heavy_groups", [P, HG], F32)
        heavy_gi = sb("heavy_gi", [P, HG], I32)
        heavy_gp = sb("heavy_gp", [P, HG], I32)
        heavy_cols = sb("heavy_cols", [P, HG], F32)
        heavy_none = sb("heavy_none", [P, HG], F32)
        agg = sb("agg", [P, NT, C], F32)
        buf_a = sb("buf_a", [P, RING_A, 2, C], F32)
        buf_b = sb("buf_b", [P, RING_B, NT - 2, C], F32)
        agg_in = sb("agg_in", [P, 2, QT, C], F32)
        h_tile = sb("h_tile", [P, 2, C], F32)
        joined_t = sb("joined_t", [P, 2, KC * P], F32)

        turned_ps = [ps(f"turned_ps{i}", [P, KC * P]) for i in range(2)]
        y_ps = [ps(f"y_ps{i}", [P, OUT]) for i in range(2)]
        before_ps = ps("before_ps", [P, NV * NT])
        total_ps = ps("total_ps", [P, NV * NT])
        ranked_ps = ps("ranked_ps", [P, NT * COLS])

        const_landed = sem("const_landed")
        const_pool = sem("const_pool")
        const_dve = sem("const_dve")
        x_landed = sem("x_landed")
        adj_landed = [sem(f"adj_landed{i}") for i in range(4)]
        signed = sem("signed")
        pack_step = sem("pack_step")
        signs_used = sem("signs_used")
        bits_packed = sem("bits_packed")
        bits_stored = sem("bits_stored")
        found_ready = sem("found_ready")
        found_step = sem("found_step")
        onehot_ready = sem("onehot_ready")
        hist_ready = sem("hist_ready")
        select_ready = sem("select_ready")
        carried_step = sem("carried_step")
        ranked_ready = sem("ranked_ready")
        norm_step = sem("norm_step")
        stats_ready = sem("stats_ready")
        std_ready = sem("std_ready")
        norm_ready = sem("norm_ready")
        h_written = sem("h_written")
        h_stored = [sem(f"h_stored{i}") for i in range(2)]
        heavy_landed = sem("heavy_landed")
        heavy_step = sem("heavy_step")
        idx_ready = sem("idx_ready")
        bufs_zeroed = sem("bufs_zeroed")
        agg_zeroed = sem("agg_zeroed")
        gathered_first = sem("gathered_first")
        gathered = [sem(f"gathered{i}") for i in range(RING_A)]
        slot_maxed = sem("slot_maxed")
        scattered = [sem(f"scattered{i}") for i in range(NQ)]
        agg_landed = [sem(f"agg_landed{i}") for i in range(2)]
        h_ready = sem("h_ready")
        turned = sem("turned")
        joined = sem("joined")
        y_ready = sem("y_ready")
        y_added = sem("y_added")
        out_stored = sem("out_stored")
        passed_pool, passed_dve, passed_act, passed_pe = [sem(f"passed_{e}") for e in ("pool", "dve", "act", "pe")]

        block = ctx.enter_context(nc.Block())

        @block.sync
        def _(sp):
            sp.dma_start(w_sb[:, :, :], w.rearrange("(k p) n -> p k n", p=P)).then_inc(const_landed, 16)
            sp.dma_start(b_sb[:, :], b.rearrange("(a n) -> a n", a=1)).then_inc(const_landed, 16)

            def load_x(nb, par):
                if due(level := value(nb, 16 * NQ, -16 * NQ)):
                    sp.wait_ge(out_stored, level)
                sp.dma_start(xs[:, par, :, :], x_rows[nb]).then_inc(x_landed, 16)

            def load_adj(nb, t0, t1):
                for t in range(t0, t1):
                    if due(level := value(nb, NT, t - 3)):
                        sp.wait_ge(signed, level)
                    sp.dma_start(adj_in[:, t % 4, :], adj_rows[nb, t]).then_inc(adj_landed[t % 4], 16)

            def load(nb, par):
                load_adj(nb, 0, 12)
                load_x(nb, par)
                load_adj(nb, 12, NT)

            load(0, 0)
            load(1, 1)
            with sp.Fori(1, B // 2) as pair:
                load(pair * 2, 0)
                load(pair * 2 + 1, 1)
            sp.wait_ge(out_stored, B * 16 * NQ)
            sp.wait_ge(bits_stored, B * 16)
            for s in h_stored:
                sp.wait_ge(s, B * 16 * NQ // 2)
            for s in scattered:
                sp.wait_ge(s, B * 16 * QT)

        @block.gpsimd
        def _(pool):
            g = nc.gpsimd
            g.iota(iota_i[:, :], pattern=[[1, P]], base=0, channel_multiplier=0).then_inc(const_pool, 1)
            g.iota(position[:, :], pattern=[[1, N]], base=0, channel_multiplier=0).then_inc(const_pool, 1)
            g.iota(row_in_tile[:, :], pattern=[[0, 1]], base=0, channel_multiplier=1,
                   allow_small_or_imprecise_dtypes=True).then_inc(const_pool, 1)
            g.memset(ident[:, :], 0.0).then_inc(const_pool, 1)
            g.memset(before[:, :], 0.0).then_inc(const_pool, 1)
            pool.wait_ge(const_pool, 5)
            g.affine_select(out=ident[:, :], in_=ident[:, :], compare_op=ALU.not_equal, fill=1.0, base=0,
                            pattern=[[-1, P]], channel_multiplier=1).then_inc(const_pool, 1)
            g.affine_select(out=before[:, :], in_=before[:, :], compare_op=ALU.is_ge, fill=1.0, base=0,
                            pattern=[[-1, P]], channel_multiplier=1).then_inc(const_pool, 1)

            def gather(dst, par, column, s):
                pool.indirect_dma_start(dst, None, h_dram[par], bass.IndirectOffsetOnAxis(ap=column, axis=0),
                                        bounds_check=N - 1, oob_is_err=False).then_inc(s, 16)

            def over_tiles(n, one, from_two=None):
                with pool.If(n > 0):
                    one(0)
                    with pool.If(n > 1):
                        one(1)
                        with pool.If(n > 2):
                            if from_two:
                                from_two()
                            one(2)
                            with pool.If(n > 3):
                                one(3)
                            with pool.If(n > 4):
                                one(4)
                                for t in range(5, 8):
                                    with pool.If(n > t):
                                        one(t)
                                with pool.If(n > 8):
                                    one(8)
                                    for t in range(9, NT):
                                        with pool.If(n > t):
                                            one(t)
                                    pool.sem_inc(passed_pool, 1)
                                pool.sem_inc(passed_pool, 1)
                            pool.sem_inc(passed_pool, 1)
                        pool.sem_inc(passed_pool, 1)
                    pool.sem_inc(passed_pool, 1)

            def heavy(i, par):
                pool.wait_ge(bits_stored, value(i, 16, 16))
                pool.sem_inc(passed_pool, 1)
                pool.wait_ge(ranked_ready, value(i, 1, 1))
                pool.sem_inc(passed_pool, 1)
                n = pool.value_load(n_tiles[0:1, par, S - 1 - LIGHT:S - LIGHT], min_val=0, max_val=NT)

                def one(t):
                    pool.indirect_dma_start(
                        heavy_bits[:, t, :], None, bits_dram,
                        bass.IndirectOffsetOnAxis(ap=perm[:, par, t:t + 1], axis=0),
                        bounds_check=N - 1, oob_is_err=False).then_inc(heavy_landed, 16)
                over_tiles(n, one)

            def scatter(b_, par):
                pool.wait_ge(slot_maxed, value(b_, NSLOT, NSLOT))
                pool.sem_inc(passed_pool, 1)
                pool.wait_ge(turned, value(b_, NT, CREDIT - NT))
                pool.sem_inc(passed_pool, 1)
                for t in range(NT):
                    pool.indirect_dma_start(
                        agg_dram[par], bass.IndirectOffsetOnAxis(ap=perm[:, par, t:t + 1], axis=0),
                        agg[:, t, :], None, bounds_check=N - 1, oob_is_err=False,
                    ).then_inc(scattered[t // QT], 16)

            def slots(i, par):
                pool.wait_ge(idx_ready, value(i, 1, 1))
                pool.sem_inc(passed_pool, 1)
                for s in h_stored:
                    pool.wait_ge(s, value(i, 8 * NQ, 8 * NQ))
                    pool.sem_inc(passed_pool, 1)
                for k in range(S):
                    n = pool.value_load(n_tiles[0:1, par, S - 1 - k:S - k], min_val=0, max_val=NT)
                    if k == 0:
                        pool.wait_ge(agg_zeroed, value(i, NQ, NQ))
                        pool.sem_inc(passed_pool, 1)
                        over_tiles(n, lambda t: gather(agg[:, t, :], par, idx[:, 0, t:t + 1], gathered_first))
                        continue
                    if k == 1:
                        pool.wait_ge(bufs_zeroed, value(i, 1, 1))
                        pool.sem_inc(passed_pool, 1)
                    if k > RING_A:
                        pool.wait_ge(slot_maxed, value(i, NSLOT, k - RING_A))
                        pool.sem_inc(passed_pool, 1)

                    def one(t):
                        dst = buf_a[:, k % RING_A, t, :] if t < 2 else buf_b[:, k % RING_B, t - 2, :]
                        gather(dst, par, idx[:, k, t:t + 1], gathered[k % RING_A])

                    def from_two():
                        if k > RING_B:
                            pool.wait_ge(slot_maxed, value(i, NSLOT, k - RING_B))
                            pool.sem_inc(passed_pool, 1)
                    over_tiles(n, one, from_two)

            def iteration(i, par, with_b=True, with_c=True):
                if with_b:
                    heavy(i, par)
                if with_c:
                    scatter(i - 1, 1 - par)
                if with_b:
                    slots(i, par)

            iteration(0, 0, with_c=False)
            with pool.Fori(0, B // 2 - 1) as pair:
                iteration(pair * 2 + 1, 1)
                iteration(pair * 2 + 2, 0)
            iteration(B - 1, 1)
            iteration(B, 0, with_b=False)

        @block.scalar
        def _(act):
            a = nc.scalar
            act.wait_ge(const_dve, 10)
            act.wait_ge(const_landed, 32)

            def zero_bufs(i):
                if due(level := value(i, NSLOT, 0)):
                    act.wait_ge(slot_maxed, level)
                    act.sem_inc(passed_act, 1)
                zb = zeros[:, :].unsqueeze(1)
                a.activation(buf_a[:, :, :, :].rearrange("p r t c -> p (r t) c"),
                             zb.to_broadcast([P, RING_A * 2, C]), ACT.Copy)
                a.activation(buf_b[:, :, :, :].rearrange("p r t c -> p (r t) c"),
                             zb.to_broadcast([P, RING_B * (NT - 2), C]), ACT.Copy).then_inc(bufs_zeroed, 1)

            def zero_agg(i):
                for q in range(NQ):
                    if due(level := value(i, 16 * QT, 0)):
                        act.wait_ge(scattered[q], level)
                    a.activation(agg[:, q * QT:(q + 1) * QT, :],
                                 zeros[:, :].unsqueeze(1).to_broadcast([P, QT, C]),
                                 ACT.Copy).then_inc(agg_zeroed, 1)

            def sign_quad(nb, q):
                if due(level := value(nb, NQ, q - 1)):
                    act.wait_ge(signs_used, level)
                for t in range(q * QT, (q + 1) * QT):
                    act.wait_ge(adj_landed[t % 4], value(nb, 16 * NT // 4, 16 * (t // 4) + 16))
                    a.activation(
                        signs[:, q % 2, t % QT, :].rearrange("p (w j e) -> p w e j", j=8, e=4),
                        adj_in[:, t % 4, :].rearrange("p (w e j) -> p w e j", e=4, j=8),
                        ACT.Sign).then_inc(signed, 1)

            def store_bits(nb):
                act.wait_ge(bits_packed, value(nb, NQ, NQ))
                act.sem_inc(passed_act, 1)
                if due(level := value(nb, 1, 0)):
                    act.wait_ge(idx_ready, level)
                    act.sem_inc(passed_act, 1)
                act.dma_start(bits_rows, bits[:, :, :]).then_inc(bits_stored, 16)

            def norm(nb, par):
                act.wait_ge(stats_ready, value(nb, 1, 1))
                a.activation(std[:, :], mean_var[:, :, 1], ACT.Sqrt, bias=eps[:, :]).then_inc(std_ready, 1)
                if due(level := value(nb, NSLOT, -NSLOT)):
                    act.wait_ge(slot_maxed, level)
                    act.sem_inc(passed_act, 1)
                act.wait_ge(norm_ready, value(nb, 1, 1))
                for q in range(NQ):
                    if due(level := value(nb, 8 * NQ, 16 * (q // 2))):
                        act.wait_ge(h_stored[q % 2], level)
                        act.sem_inc(passed_act, 1)
                    for t in range(q * QT, (q + 1) * QT):
                        a.activation(h_out[:, q % 2, t % QT, :], xs[:, par, t, :], ACT.Relu,
                                     bias=shift[:, par, t:t + 1], scale=rstd[:, par, t:t + 1]).then_inc(h_written, 1)
                    act.wait_ge(h_written, value(nb, NT, (q + 1) * QT))
                    act.sem_inc(passed_act, 1)
                    act.dma_start(h_rows[par][:, q * QT:(q + 1) * QT, :], h_out[:, q % 2, :, :]).then_inc(h_stored[q % 2], 16)

            def load_agg(b_, par, q):
                if q == 0:
                    for s in scattered:
                        act.wait_ge(s, value(b_, 16 * QT, 16 * QT))
                        act.sem_inc(passed_act, 1)
                act.wait_ge(turned, value(b_, NT, QT * (q - 1) + CREDIT))
                act.sem_inc(passed_act, 1)
                act.dma_start(agg_in[:, q % 2, :, :], agg_rows[par][:, q * QT:(q + 1) * QT, :]).then_inc(agg_landed[q % 2], 16)

            def h_again(b_, par, t):
                act.wait_ge(turned, value(b_, NT, t - 1 + CREDIT))
                a.activation(h_tile[:, t % 2, :], xs[:, par, t, :], ACT.Relu, bias=shift[:, par, t:t + 1],
                             scale=rstd[:, par, t:t + 1]).then_inc(h_ready, 1)

            def join(b_, t):
                act.wait_ge(y_ready, value(b_, NT, t - 1 + CREDIT))
                act.wait_ge(turned, value(b_, NT, t + 1 + CREDIT))
                act.sem_inc(passed_act, 1)
                a.activation(joined_t[:, t % 2, :], turned_ps[t % 2][:, :], ACT.Copy).then_inc(joined, 1)

            def store_out(b_, par, q):
                act.wait_ge(y_added, value(b_, NT, (q + 1) * QT + CREDIT))
                act.sem_inc(passed_act, 1)
                act.dma_start(out_rows[b_, :, q * QT:(q + 1) * QT, :],
                              xs[:, par, q * QT:(q + 1) * QT, :]).then_inc(out_stored, 16)

            def tiles_c(b_, par, t0, t1):
                for t in range(t0, t1):
                    if t % QT == 0:
                        load_agg(b_, par, t // QT)
                    if t == t0:
                        h_again(b_, par, t)
                    if t + 1 < t1:
                        h_again(b_, par, t + 1)
                    join(b_, t)
                for q in range(t0 // QT, t1 // QT):
                    store_out(b_, par, q)

            def iteration(i, par, with_a=True, with_b=True, with_c=True):
                if with_b:
                    zero_bufs(i)
                if with_a:
                    sign_quad(i + 1, 0)
                if with_b:
                    zero_agg(i)
                if with_a:
                    sign_quad(i + 1, 1)
                if with_c:
                    tiles_c(i - 1, 1 - par, 0, NT // 2)
                if with_a:
                    sign_quad(i + 1, 2)
                if with_c:
                    tiles_c(i - 1, 1 - par, NT // 2, NT)
                if with_a:
                    sign_quad(i + 1, 3)
                    store_bits(i + 1)
                    norm(i + 1, 1 - par)

            act.sem_inc(joined, CREDIT)
            iteration(-1, 1, with_b=False, with_c=False)
            iteration(0, 0, with_c=False)
            with act.Fori(0, B // 2 - 1) as pair:
                iteration(pair * 2 + 1, 1)
                iteration(pair * 2 + 2, 0)
            iteration(B - 1, 1, with_a=False)
            iteration(B, 0, with_a=False, with_b=False)

        @block.tensor
        def _(pe):
            pe.wait_ge(const_pool, 7)
            pe.wait_ge(const_dve, 10)
            pe.wait_ge(const_landed, 32)

            def turn(b_, t):
                pe.wait_ge(joined, value(b_, NT, t - 1 + CREDIT))
                pe.wait_ge(h_ready, value(b_, NT, t + 1))
                pe.sem_inc(passed_pe, 1)
                if t % QT == 0:
                    pe.wait_ge(agg_landed[t // QT % 2], value(b_, 8 * NQ, 16 * (t // QT // 2) + 16))
                    pe.sem_inc(passed_pe, 1)
                for c in range(KC):
                    src = h_tile[:, t % 2, c * P:(c + 1) * P] if c < 2 else agg_in[:, t // QT % 2, t % QT, (c - 2) * P:(c - 1) * P]
                    last = nc.tensor.transpose(turned_ps[t % 2][:, c * P:(c + 1) * P], src, ident[:, :])
                last.then_inc(turned, 1)

            def multiply(b_, t):
                pe.wait_ge(y_added, value(b_, NT, t - 1 + CREDIT))
                pe.wait_ge(joined, value(b_, NT, t + 1 + CREDIT))
                pe.sem_inc(passed_pe, 1)
                nc.tensor.matmul(y_ps[t % 2][:, :], ones_f[0:1, 0:P], b_sb[:, :], start=True, stop=False)
                for c in range(KC):
                    last = nc.tensor.matmul(y_ps[t % 2][:, :], joined_t[:, t % 2, c * P:(c + 1) * P], w_sb[:, c, :],
                                            start=False, stop=(c == KC - 1))
                last.then_inc(y_ready, 1)

            def products(b_):
                for half in range(2):
                    for t in range(half * NT // 2, (half + 1) * NT // 2):
                        turn(b_, t)
                        if t % (NT // 2):
                            multiply(b_, t - 1)
                    multiply(b_, t)

            def rank_rows(nb):
                pe.wait_ge(onehot_ready, value(nb, 1, 1))
                flat = onehot[:, :, :].rearrange("p v t -> p (v t)")
                nc.tensor.matmul(before_ps[:, :], before[:, :], flat, start=True, stop=True)
                nc.tensor.matmul(total_ps[:, :], ones_bf[:, :], flat, start=True, stop=True).then_inc(hist_ready, 1)
                for s in range(NT):
                    pe.wait_ge(select_ready, value(nb, NT, s + 1))
                    for d in range(NT):
                        last = nc.tensor.matmul(
                            ranked_ps[:, d * COLS:(d + 1) * COLS], select[:, s % 2, d * P:(d + 1) * P],
                            carried[:, s, :], start=(s == 0 and d == 0), stop=(s == NT - 1), skip_group_check=True)
                    last.then_inc(carried_step, 1)

            pe.sem_inc(turned, CREDIT)
            pe.sem_inc(y_ready, CREDIT)
            rank_rows(0)
            rank_rows(1)
            with pe.Fori(0, B // 2 - 1) as pair:
                products(pair * 2)
                rank_rows(pair * 2 + 2)
                products(pair * 2 + 1)
                rank_rows(pair * 2 + 3)
            products(B - 2)
            products(B - 1)

        @block.vector
        def _(dve):
            v = nc.vector
            total_first = dve.alloc_register("total_first")
            totals = [dve.alloc_register(f"total{i}") for i in range(RING_A)]
            heavy_total = dve.alloc_register("heavy_total")
            heavy_done = dve.alloc_register("heavy_done")
            for r in (total_first, *totals, heavy_total, heavy_done):
                dve.reg_mov(r, 0)

            def read(r):
                return dve.snap(r, min_val=0, max_val=60000)

            v.memset(zeros[:, :], 0.0)
            v.memset(ones_f[:, :], 1.0)
            v.memset(ones_bf[:, :], 1.0)
            v.memset(eps[:, :], EPS)
            for i in range(GROUP):
                v.memset(bit_of[:, i:i + 1], 1 << i)
                v.memset(pick[:, i:i + 1], (1 << (7 + i)) | 127)
                v.memset(bit_late[:, i:i + 1], float(GROUP - i))
            for t in range(NT):
                ins = v.memset(tile_no[:, t:t + 1], float(t))
            ins.then_inc(const_dve, 1)
            dve.wait_ge(const_pool, 7)
            v.tensor_copy(group_no[:, :], iota_i[:, :]).then_inc(const_dve, 1)
            dve.wait_ge(const_dve, 2)
            v.tensor_scalar(group_late[:, :], group_no[:, :], -65536.0, 65536.0 * (NG - 1), ALU.mult,
                            ALU.add).then_inc(const_dve, 1)
            v.tensor_scalar(counts_down[:, :], group_no[:, 0:NV], -1.0, float(S), ALU.mult,
                            ALU.add).then_inc(const_dve, 1)
            for t in range(NT):
                ins = v.tensor_copy(carried[:, t, 2 * LIGHT:2 * LIGHT + 1], row_in_tile[:, :])
            ins.then_inc(const_dve, 1)
            v.tensor_copy(carried[:, :, 2 * LIGHT + 1], tile_no[:, :]).then_inc(const_dve, 5)
            dve.sem_inc(y_added, CREDIT)

            PACK = 7

            def pack_quad(nb, q):
                def step(n):
                    return value(nb, PACK * NQ, PACK * q + n)
                s = signs[:, q % 2, :, :].rearrange("p t n -> p (t n)").bitcast(U32)
                dve.wait_ge(signed, value(nb, NT, (q + 1) * QT))
                v.tensor_scalar(s, s, 0x01010101, None, ALU.bitwise_and).then_inc(pack_step, 1)
                if due(level := value(nb, NQ, q)):
                    dve.wait_ge(found_ready, level)
                    dve.sem_inc(passed_dve, 1)
                dve.wait_ge(pack_step, step(1))
                two = s.rearrange("p (n two) -> p n two", two=2)
                v.scalar_tensor_tensor(half1, two[:, :, 1], 1, two[:, :, 0], ALU.logical_shift_left,
                                       ALU.bitwise_or).then_inc(pack_step, 1)
                dve.wait_ge(pack_step, step(2))
                dve.sem_inc(passed_dve, 1)
                dve.sem_inc(signs_used, 1)
                two = half1.rearrange("p (n two) -> p n two", two=2)
                v.scalar_tensor_tensor(half2, two[:, :, 1], 2, two[:, :, 0], ALU.logical_shift_left,
                                       ALU.bitwise_or).then_inc(pack_step, 1)
                if q == 0:
                    if due(level := value(nb, 16, 0)):
                        dve.wait_ge(bits_stored, level)
                dve.wait_ge(pack_step, step(3))
                dve.sem_inc(passed_dve, 1)
                two = half2.rearrange("p (n two) -> p n two", two=2)
                quad = bits[:, q * QT:(q + 1) * QT, :]
                v.scalar_tensor_tensor(quad.rearrange("p t w -> p (t w)"), two[:, :, 1], 4, two[:, :, 0],
                                       ALU.logical_shift_left, ALU.bitwise_or).then_inc(pack_step, 1)
                dve.wait_ge(pack_step, step(4))
                dve.sem_inc(passed_dve, 1)
                dve.sem_inc(bits_packed, 1)
                v.scalar_tensor_tensor(keys[:, :, :], quad.bitcast(U16), 128.0,
                                       group_no[:, :].unsqueeze(1).to_broadcast([P, QT, NG]),
                                       ALU.mult, ALU.add).then_inc(pack_step, 1)
                dve.wait_ge(pack_step, step(5))
                dve.sem_inc(passed_dve, 1)
                for t in range(QT):
                    ins = v.max(top_groups[:, t, :], keys[:, t, :])
                ins.then_inc(pack_step, 1)
                dve.wait_ge(pack_step, step(6))
                v.tensor_tensor(cand[:, :, :, :].rearrange("p t g i -> p (t g) i"),
                                top_groups[:, :, :].rearrange("p t g -> p (t g)").unsqueeze(2).to_broadcast([P, QT * 8, GROUP]),
                                pick[:, :].unsqueeze(1).to_broadcast([P, QT * 8, GROUP]),
                                ALU.bitwise_and).then_inc(pack_step, 1)
                dve.wait_ge(pack_step, step(7))
                dve.sem_inc(passed_dve, 1)
                for t in range(QT):
                    ins = v.max(found[:, q * QT + t, :], cand[:, t, :, :].rearrange("p g i -> p (g i)"))
                ins.then_inc(found_ready, 1)

            NORM = 3

            def layernorm(nb, par):
                dve.wait_ge(x_landed, value(nb, 16, 16))
                dve.sem_inc(passed_dve, 1)
                for t in range(NT):
                    ins = v.bn_stats(stats[:, t, :], xs[:, par, t, :])
                ins.then_inc(norm_step, 1)
                dve.wait_ge(norm_step, value(nb, NORM, 1))
                dve.sem_inc(passed_dve, 1)
                if due(level := value(nb, 1, 0)):
                    dve.wait_ge(std_ready, level)
                    dve.sem_inc(passed_dve, 1)
                for t in range(NT):
                    ins = v.bn_aggr(mean_var[:, t, :], stats[:, t, :])
                ins.then_inc(stats_ready, 1)
                if due(level := value(nb, NT, -NT)):
                    dve.wait_ge(h_ready, level)
                    dve.sem_inc(passed_dve, 1)
                dve.wait_ge(std_ready, value(nb, 1, 1))
                v.reciprocal(rstd[:, par, :], std[:, :]).then_inc(norm_step, 1)
                dve.wait_ge(norm_step, value(nb, NORM, 2))
                v.scalar_tensor_tensor(shift[:, par, :], mean_var[:, :, 0], -1.0, rstd[:, par, :], ALU.mult,
                                       ALU.mult).then_inc(norm_step, 1)
                dve.wait_ge(norm_step, value(nb, NORM, 3))
                dve.sem_inc(passed_dve, 1)
                dve.sem_inc(norm_ready, 1)

            RANK = 32

            def rank_batch(nb, par):
                steps = Steps(nb * RANK)

                f2 = found[:, :, :].rearrange("p t k -> p (t k)")
                dve.wait_ge(found_ready, value(nb, NQ, NQ))
                dve.sem_inc(passed_dve, 1)
                v.tensor_copy(found_f[:, :], f2).then_inc(found_step, steps.up())
                dve.wait_ge(found_step, steps.now)
                dve.sem_inc(passed_dve, 1)
                v.tensor_scalar(found_f[:, :].bitcast(I32), found_f[:, :].bitcast(I32), 23, None,
                                     ALU.logical_shift_right).then_inc(found_step, steps.up())
                v.tensor_scalar(f2, f2, 127, None, ALU.bitwise_and).then_inc(found_step, steps.up())
                dve.wait_ge(found_step, steps.now)
                dve.sem_inc(passed_dve, 1)
                if due(level := value(nb, NT, 0)):
                    dve.wait_ge(carried_step, level)
                v.tensor_copy(carried[:, :, 0:LIGHT], found[:, :, :]).then_inc(found_step, steps.up())
                v.tensor_scalar(carried[:, :, LIGHT:2 * LIGHT],
                                     found_f[:, :].bitcast(I32).rearrange("p (t k) -> p t k", k=8),
                                     -133.0, 0.0, ALU.add, ALU.max).then_inc(found_step, steps.up())

                half = bits[:, :, :].rearrange("p t w -> p (t w)").bitcast(U16)
                pa, pb = pop_a, pop_b
                v.tensor_scalar(pa, half, 1, 0x5555, ALU.logical_shift_right, ALU.bitwise_and).then_inc(found_step, steps.up())
                dve.wait_ge(found_step, steps.now)
                dve.sem_inc(passed_dve, 1)
                v.tensor_tensor(pb, half, pa, ALU.subtract).then_inc(found_step, steps.up())
                dve.wait_ge(found_step, steps.now)
                dve.sem_inc(passed_dve, 1)
                v.tensor_scalar(pa, pb, 2, 0x3333, ALU.logical_shift_right, ALU.bitwise_and).then_inc(found_step, steps.up())
                dve.wait_ge(found_step, steps.now)
                dve.sem_inc(passed_dve, 1)
                v.tensor_scalar(pb, pb, 0x3333, None, ALU.bitwise_and).then_inc(found_step, steps.up())
                dve.wait_ge(found_step, steps.now)
                dve.sem_inc(passed_dve, 1)
                v.tensor_tensor(pa, pa, pb, ALU.add).then_inc(found_step, steps.up())
                dve.wait_ge(found_step, steps.now)
                dve.sem_inc(passed_dve, 1)
                v.tensor_scalar(pb, pa, 4, 0x0F0F, ALU.logical_shift_right, ALU.bitwise_and).then_inc(found_step, steps.up())
                v.tensor_scalar(pa, pa, 0x0F0F, None, ALU.bitwise_and).then_inc(found_step, steps.up())
                dve.wait_ge(found_step, steps.now)
                dve.sem_inc(passed_dve, 1)
                v.tensor_tensor(pb, pa, pb, ALU.add).then_inc(found_step, steps.up())
                dve.wait_ge(found_step, steps.now)
                dve.sem_inc(passed_dve, 1)
                n = NG
                src, dst = pop_b, pop_a
                while n > 8:
                    sv = src[:, 0:NT * n].rearrange("p (t h n) -> p t h n", t=NT, h=2)
                    dv = dst[:, 0:NT * n // 2].rearrange("p (t n) -> p t n", t=NT)
                    v.tensor_tensor(dv, sv[:, :, 0, :], sv[:, :, 1, :], ALU.add).then_inc(found_step, steps.up())
                    dve.wait_ge(found_step, steps.now)
                    dve.sem_inc(passed_dve, 1)
                    src, dst, n = dst, src, n // 2
                v.tensor_reduce(count[:, :], src[:, 0:NT * n].bitcast(U8).rearrange("p (t n) -> p t n", t=NT),
                                     AX_X, ALU.add).then_inc(found_step, steps.up())
                dve.wait_ge(found_step, steps.now)
                dve.sem_inc(passed_dve, 1)
                v.tensor_scalar(count[:, :], count[:, :], float(S), None, ALU.min).then_inc(found_step, steps.up())
                dve.wait_ge(found_step, steps.now)
                dve.sem_inc(passed_dve, 1)
                if due(level := value(nb, 1, 0)):
                    dve.wait_ge(hist_ready, level)
                v.tensor_tensor(onehot[:, :, :], count[:, :].unsqueeze(1).to_broadcast([P, NV, NT]),
                                counts_down[:, :].unsqueeze(2).to_broadcast([P, NV, NT]),
                                ALU.is_equal).then_inc(onehot_ready, 1)
                dve.wait_ge(hist_ready, value(nb, 1, 1))
                v.tensor_tensor_scan(cum[:, :], ones_f[:, :], total_ps[:, :], 0.0, ALU.mult, ALU.add).then_inc(found_step, steps.up())
                dve.wait_ge(found_step, steps.now)
                dve.sem_inc(passed_dve, 1)
                v.tensor_tensor(spot[:, :], cum[:, :], total_ps[:, :], ALU.subtract).then_inc(found_step, steps.up())
                dve.wait_ge(found_step, steps.now)
                dve.sem_inc(passed_dve, 1)
                v.tensor_tensor(spot[:, :], spot[:, :], before_ps[:, :], ALU.add).then_inc(found_step, steps.up())
                dve.wait_ge(found_step, steps.now)
                dve.sem_inc(passed_dve, 1)
                v.tensor_tensor(spot[:, :], spot[:, :], onehot[:, :, :].rearrange("p v t -> p (v t)"), ALU.mult).then_inc(found_step, steps.up())
                dve.wait_ge(found_step, steps.now)
                dve.sem_inc(passed_dve, 1)
                v.tensor_reduce(rank[:, :], spot[:, :].rearrange("p (v t) -> p t v", v=NV), AX_X, ALU.add).then_inc(found_step, steps.up())
                dve.wait_ge(found_step, steps.now)
                dve.sem_inc(passed_dve, 1)
                for s in range(NT):
                    if due(level := value(nb, NT, s - 1)):
                        dve.wait_ge(carried_step, level)
                    v.tensor_scalar(select[:, s % 2, :], position[:, :], rank[:, s:s + 1], None,
                                    ALU.is_equal).then_inc(select_ready, 1)
                for s in scattered:
                    if due(level := value(nb, 16 * QT, -16 * QT)):
                        dve.wait_ge(s, level)
                        dve.sem_inc(passed_dve, 1)
                v.tensor_scalar(tiles_f[:, :], cum[:, :].rearrange("p (v t) -> p v t", v=NV)[:, 0:S, NT - 1],
                                     float(P - 1), None, ALU.add).then_inc(found_step, steps.up())
                dve.wait_ge(found_step, steps.now)
                dve.sem_inc(passed_dve, 1)
                v.tensor_scalar(n_tiles[:, par, :], tiles_f[:, :], 7, None, ALU.logical_shift_right).then_inc(found_step, steps.up())
                dve.wait_ge(carried_step, value(nb, NT, NT))
                v.tensor_copy(ranked[:, :, :].rearrange("p t c -> p (t c)"), ranked_ps[:, :]).then_inc(found_step, steps.up())
                dve.wait_ge(found_step, steps.now)
                dve.sem_inc(passed_dve, 1)
                group, bit1 = ranked[:, :, 0:LIGHT], ranked[:, :, LIGHT:2 * LIGHT]
                so = slot_of[:, :].rearrange("p (t k) -> p t k", k=8)
                no = no_slot[:, :].rearrange("p (t k) -> p t k", k=8)
                v.scalar_tensor_tensor(so, group, float(GROUP), bit1, ALU.mult, ALU.add).then_inc(found_step, steps.up())
                v.tensor_scalar(no, bit1, 0.0, float(SKIP), ALU.is_equal, ALU.mult).then_inc(found_step, steps.up())
                v.scalar_tensor_tensor(row_of[:, :], ranked[:, :, 2 * LIGHT + 1], float(P),
                                            ranked[:, :, 2 * LIGHT], ALU.mult, ALU.add).then_inc(found_step, steps.up())
                dve.wait_ge(found_step, steps.now)
                dve.sem_inc(passed_dve, 1)
                v.scalar_tensor_tensor(idx[:, 0:LIGHT, :].rearrange("p k t -> p t k"), so, -1.0, no,
                                            ALU.add, ALU.add).then_inc(found_step, steps.up())
                v.tensor_copy(perm[:, par, :], row_of[:, :]).then_inc(found_step, steps.up())
                dve.wait_ge(found_step, steps.now)
                dve.sem_inc(passed_dve, 1)
                dve.sem_inc(ranked_ready, 1)
                assert steps.n == RANK, steps.n

            HEAVY = 23

            def heavy_tile(d):
                steps = Steps(read(heavy_done))

                half = heavy_bits[:, bass.ds(d, 1), :].rearrange("p t w -> p (t w)").bitcast(U16)
                v.scalar_tensor_tensor(heavy_key[:, :], half, 0.0, group_late[:, :], ALU.is_gt, ALU.mult).then_inc(heavy_step, steps.up())
                dve.wait_ge(heavy_step, steps.now)
                dve.sem_inc(passed_dve, 1)
                v.tensor_tensor(heavy_key[:, :], heavy_key[:, :], half, ALU.add).then_inc(heavy_step, steps.up())
                dve.wait_ge(heavy_step, steps.now)
                dve.sem_inc(passed_dve, 1)
                for r in range(HG // 8):
                    eight = heavy_groups[:, 8 * r:8 * r + 8]
                    v.max(eight, heavy_key[:, :]).then_inc(heavy_step, steps.up())
                    dve.wait_ge(heavy_step, steps.now)
                    dve.sem_inc(passed_dve, 1)
                    if r < HG // 8 - 1:
                        v.match_replace(heavy_key[:, :], eight, heavy_key[:, :], 0.0).then_inc(heavy_step, steps.up())
                        dve.wait_ge(heavy_step, steps.now)
                        dve.sem_inc(passed_dve, 1)
                v.tensor_copy(heavy_gi[:, :], heavy_groups[:, :]).then_inc(heavy_step, steps.up())
                dve.wait_ge(heavy_step, steps.now)
                dve.sem_inc(passed_dve, 1)
                v.tensor_scalar(heavy_gp[:, :], heavy_gi[:, :], 16, 4, ALU.logical_shift_right, ALU.logical_shift_left).then_inc(heavy_step, steps.up())
                v.tensor_tensor(heavy_bit[:, :, :], heavy_gi[:, :].unsqueeze(2).to_broadcast([P, HG, GROUP]),
                                     bit_of[:, :].unsqueeze(1).to_broadcast([P, HG, GROUP]), ALU.bitwise_and).then_inc(heavy_step, steps.up())
                dve.wait_ge(heavy_step, steps.now)
                dve.sem_inc(passed_dve, 1)
                v.tensor_tensor(heavy_pos[:, :, :], heavy_gp[:, :].unsqueeze(2).to_broadcast([P, HG, GROUP]),
                                     bit_late[:, :].unsqueeze(1).to_broadcast([P, HG, GROUP]), ALU.add).then_inc(heavy_step, steps.up())
                dve.wait_ge(heavy_step, steps.now)
                dve.sem_inc(passed_dve, 1)
                pos = heavy_pos[:, :, :].rearrange("p g i -> p (g i)")
                v.scalar_tensor_tensor(pos, heavy_bit[:, :, :].rearrange("p g i -> p (g i)"), 0.0, pos,
                                            ALU.is_gt, ALU.mult).then_inc(heavy_step, steps.up())
                dve.wait_ge(heavy_step, steps.now)
                dve.sem_inc(passed_dve, 1)
                for r in range(4):
                    eight = heavy_cols[:, 8 * r:8 * r + 8]
                    v.max(eight, pos).then_inc(heavy_step, steps.up())
                    dve.wait_ge(heavy_step, steps.now)
                    dve.sem_inc(passed_dve, 1)
                    if r < 3:
                        v.match_replace(pos, eight, pos, 0.0).then_inc(heavy_step, steps.up())
                        dve.wait_ge(heavy_step, steps.now)
                        dve.sem_inc(passed_dve, 1)
                v.tensor_scalar(heavy_none[:, :], heavy_cols[:, :], 0.0, float(SKIP), ALU.is_equal, ALU.mult).then_inc(heavy_step, steps.up())
                dve.wait_ge(heavy_step, steps.now)
                dve.sem_inc(passed_dve, 1)
                v.scalar_tensor_tensor(idx[:, :, bass.ds(d, 1)].rearrange("p k t -> p (k t)"), heavy_none[:, 0:S],
                                            float(N), heavy_cols[:, 0:S], ALU.add, ALU.subtract).then_inc(heavy_step, steps.up())
                assert steps.n == HEAVY, steps.n
                dve.reg_add(heavy_done, heavy_done, HEAVY)
                dve.wait_ge(heavy_step, read(heavy_done))
                dve.sem_inc(passed_dve, 1)

            def heavy_rows(i, par):
                n = dve.value_load(n_tiles[0:1, par, S - 1 - LIGHT:S - LIGHT], min_val=0, max_val=NT)
                dve.reg_add(heavy_total, heavy_total, n * 16)
                with dve.If(n > 0):
                    dve.wait_ge(heavy_landed, read(heavy_total))
                    dve.sem_inc(passed_dve, 1)
                    with dve.Fori(0, n) as d:
                        heavy_tile(d)
                    dve.sem_inc(passed_dve, 1)
                dve.sem_inc(idx_ready, 1)

            def maxed(lo, hi, k):
                src = buf_a[:, k % RING_A, lo:hi, :] if hi <= 2 else buf_b[:, k % RING_B, lo - 2:hi - 2, :]
                dst = agg[:, lo:hi, :]
                return v.tensor_tensor(dst, dst, src, ALU.max)

            def slot(i, par, k):
                n = dve.value_load(n_tiles[0:1, par, S - 1 - k:S - k], min_val=0, max_val=NT)
                if k == 1:
                    n0 = dve.value_load(n_tiles[0:1, par, S - 1:S], min_val=0, max_val=NT)
                    dve.reg_add(total_first, total_first, n0 * 16)
                    dve.wait_ge(agg_zeroed, value(i, NQ, NQ))
                    dve.sem_inc(passed_dve, 1)
                    dve.wait_ge(bufs_zeroed, value(i, 1, 1))
                    dve.sem_inc(passed_dve, 1)
                    with dve.If(n0 > 0):
                        dve.wait_ge(gathered_first, read(total_first))
                        dve.sem_inc(passed_dve, 1)
                total = totals[k % RING_A]
                dve.reg_add(total, total, n * 16)
                if due(level := value(i, NSLOT, k - 1)):
                    dve.wait_ge(slot_maxed, level)
                    dve.sem_inc(passed_dve, 1)
                with dve.If(n > 0):
                    dve.wait_ge(gathered[k % RING_A], read(total))
                    dve.sem_inc(passed_dve, 1)
                    with dve.If(n > 1):
                        with dve.If(n > 2):
                            with dve.If(n > 4):
                                with dve.If(n > 8):
                                    maxed(8, NT, k)
                                maxed(4, 8, k)
                            maxed(2, 4, k)
                        maxed(1, 2, k)
                    dve.sem_inc(passed_dve, 1)
                maxed(0, 1, k).then_inc(slot_maxed, 1)

            def add_x(b_, par, t0, t1):
                for t in range(t0, t1):
                    dve.wait_ge(y_ready, value(b_, NT, t + 1 + CREDIT))
                    v.scalar_tensor_tensor(xs[:, par, t, :], y_ps[t % 2][:, :], 0.0, xs[:, par, t, :], ALU.max,
                                           ALU.add).then_inc(y_added, 1)

            def iteration(i, par, with_a=True, with_b=True, with_c=True):
                nb, other = i + 1, 1 - par
                if with_b:
                    heavy_rows(i, par)
                if with_a:
                    pack_quad(nb, 0)
                if with_b:
                    slot(i, par, 1)
                if with_a:
                    pack_quad(nb, 1)
                if with_b:
                    slot(i, par, 2)
                if with_c:
                    add_x(i - 1, other, 0, NT // 2)
                if with_b:
                    slot(i, par, 3)
                if with_a:
                    pack_quad(nb, 2)
                if with_b:
                    slot(i, par, 4)
                if with_c:
                    add_x(i - 1, other, NT // 2, NT)
                if with_b:
                    slot(i, par, 5)
                if with_a:
                    pack_quad(nb, 3)
                if with_b:
                    slot(i, par, 6)
                if with_a:
                    layernorm(nb, other)
                if with_b:
                    for k in range(7, S):
                        slot(i, par, k)
                if with_a:
                    rank_batch(nb, other)

            iteration(-1, 1, with_b=False, with_c=False)
            iteration(0, 0, with_c=False)
            with dve.Fori(0, B // 2 - 1) as pair:
                iteration(pair * 2 + 1, 1)
                iteration(pair * 2 + 2, 0)
            iteration(B - 1, 1, with_a=False)
            iteration(B, 0, with_a=False, with_b=False)


_INS = ["x", "adj", "L0_gnn_W", "L0_gnn_b"]


def kernel(**inputs):
    import numpy as _np
    import concourse.bacc as _bacc
    from concourse import mybir as _mybir
    from concourse.bass_utils import run_bass_kernel_spmd as _run

    nc = _bacc.Bacc("TRN2", target_bir_lowering=False, num_devices=1)
    arrays, args = {}, []
    for name in _INS:
        a = _np.ascontiguousarray(inputs[name])
        arrays[f"in_{name}_dram"] = a
        args.append(nc.dram_tensor(f"in_{name}_dram", a.shape, _mybir.dt.from_np(a.dtype), kind="ExternalInput").ap())
    shape = tuple(inputs["x"].shape)
    args.append(nc.dram_tensor("out_dram", shape, _mybir.dt.float32, kind="ExternalOutput").ap())
    build(nc, *args)
    r = _run(nc, [arrays], core_ids=[0])
    return r.results[0]["out_dram"]
```

```python
from contextlib import ExitStack

import concourse.bass as bass
from concourse import mybir

ALU = mybir.AluOpType
ACT = mybir.ActivationFunctionType
F32 = mybir.dt.float32
BF16 = mybir.dt.bfloat16
I32 = mybir.dt.int32
U32 = mybir.dt.uint32
I16 = mybir.dt.int16
U16 = mybir.dt.uint16
I8 = mybir.dt.int8
U8 = mybir.dt.uint8
AX_X = mybir.AxisListType.X

P = 128
S = 25
LIGHT = 8
GROUP = 16
QT = 4
RING_A, RING_B = 8, 2
SINGLE = 8
RING_ADJ, RING_AGG = 3, 3
SKIP = 1 << 20
CREDIT = 32
EPS = 1e-5


def value(batch, per_batch, more):
    return batch * per_batch + more


def due(level):
    return not isinstance(level, int) or level > 0


def user_before(n, ring, per_batch):
    return n - ring if n >= ring else range(n, per_batch, ring)[-1] - per_batch


class Steps:

    def __init__(self, base):
        self.base, self.n = base, 0

    def up(self):
        self.n += 1
        return 1

    @property
    def now(self):
        return self.base + self.n


def build(nc, x, adj, w, b, out):
    B, N, C = x.shape
    OUT = w.shape[1]
    NT = N // P
    NQ = NT // QT
    NG = N // GROUP
    WORDS = N // 32
    KC = 2 * C // P
    NV = S + 1
    NSLOT = S - 1
    NGRP = (NSLOT - SINGLE) // 4
    COLS = 2 * LIGHT + 2
    HG = S
    assert NT == 16 and NG == P and C == OUT == 256 and KC == 4

    x_rows = x.rearrange("b (t p) c -> b p t c", p=P)
    out_rows = out.rearrange("b (t p) c -> b p t c", p=P)
    adj_rows = adj.rearrange("b (t p) j -> b t p j", p=P)
    h_dram = [nc.dram_tensor(f"h_table{i}", [N, C], F32).ap() for i in range(2)]
    agg_dram = [nc.dram_tensor(f"agg_table{i}", [N, C], F32).ap() for i in range(2)]
    bits_dram = nc.dram_tensor("bits_table", [N, WORDS], U32).ap()
    h_rows = [d.rearrange("(t p) c -> p t c", p=P) for d in h_dram]
    agg_rows = [d.rearrange("(t p) c -> p t c", p=P) for d in agg_dram]
    bits_rows = bits_dram.rearrange("(t p) j -> p t j", p=P)

    with ExitStack() as ctx:
        def sb(name, shape, dt):
            return ctx.enter_context(nc.sbuf_tensor(name, shape, dt))

        def ps(name, shape):
            return ctx.enter_context(nc.psum_tensor(name, shape, F32))

        def sem(name):
            return ctx.enter_context(nc.semaphore(name))

        ident = sb("ident", [P, P], F32)
        before = sb("before", [P, P], BF16)
        ones_bf = sb("ones_bf", [P, P], BF16)
        ones_f = sb("ones_f", [P, NV * NT], F32)
        zeros = sb("zeros", [P, C], F32)
        eps = sb("eps", [P, 1], F32)
        w_sb = sb("w_sb", [P, KC, OUT], F32)
        b_sb = sb("b_sb", [1, OUT], F32)
        position = sb("position", [P, N], I16)
        group_no = sb("group_no", [P, NG], F32)
        group_late = sb("group_late", [P, NG], F32)
        bit_late = sb("bit_late", [P, GROUP], F32)
        bit_of = sb("bit_of", [P, GROUP], I32)
        pick = sb("pick", [P, GROUP], I32)
        counts_down = sb("counts_down", [P, NV], F32)
        iota_i = sb("iota_i", [P, P], I32)
        row_in_tile = sb("row_in_tile", [P, 1], F32)
        tile_no = sb("tile_no", [P, NT], F32)

        xs = sb("xs", [P, 2, NT, C], F32)
        adj_in = sb("adj_in", [P, RING_ADJ, N], I32)
        signs = sb("signs", [P, 2, QT, N], I8)
        work_a = sb("work_a", [P, QT * N // 8], U32)
        work_b = sb("work_b", [P, QT * N // 8], U32)
        half1 = work_a[:, :]
        half2 = work_b[:, 0:QT * N // 16]
        keys = work_b[:, QT * NG:2 * QT * NG].bitcast(I32).rearrange("p (t g) -> p t g", t=QT)
        cand = work_a[:, 0:QT * 8 * GROUP].bitcast(I32).rearrange("p (t g i) -> p t g i", t=QT, g=8)
        pop_a = work_a[:, :].bitcast(U16)
        pop_b = work_b[:, :].bitcast(U16)
        heavy_bit = work_a[:, 0:2 * HG * GROUP].bitcast(I32).rearrange("p (g i) -> p g i", i=GROUP)
        heavy_pos = work_b[:, 0:2 * HG * GROUP].bitcast(F32).rearrange("p (g i) -> p g i", i=GROUP)
        bits = sb("bits", [P, NT, WORDS], U32)
        top_groups = sb("top_groups", [P, QT, 8], I32)
        found = sb("found", [P, NT, 8], I32)
        found_f = sb("found_f", [P, NT * 8], F32)
        carried = sb("carried", [P, NT, COLS], BF16)
        count = sb("count", [P, NT], F32)
        onehot = sb("onehot", [P, NV, NT], BF16)
        cum = sb("cum", [P, NV * NT], F32)
        spot = sb("spot", [P, NV * NT], F32)
        rank = sb("rank", [P, NT], F32)
        select = sb("select", [P, 2, N], BF16)
        tiles_f = sb("tiles_f", [P, S + 1], I32)
        n_tiles = sb("n_tiles", [P, 2, S + 1], I32)
        ranked = sb("ranked", [P, NT, COLS], F32)
        slot_of = sb("slot_of", [P, NT * 8], F32)
        no_slot = sb("no_slot", [P, NT * 8], F32)
        row_of = sb("row_of", [P, NT], F32)
        perm = sb("perm", [P, 2, NT], U32)
        idx = sb("idx", [P, 2, S, NT], U32)
        stats = sb("stats", [P, NT, 6], F32)
        mean_var = sb("mean_var", [P, NT, 2], F32)
        std = sb("std", [P, NT], F32)
        rstd = sb("rstd", [P, 2, NT], F32)
        shift = sb("shift", [P, 2, NT], F32)
        h_out = sb("h_out", [P, 2, 2, C], F32)
        heavy_bits = sb("heavy_bits", [P, NT, WORDS], U32)
        heavy_key = sb("heavy_key", [P, 2, NG], F32)
        heavy_groups = sb("heavy_groups", [P, 2, 32], F32)
        heavy_gi = sb("heavy_gi", [P, 2 * HG], I32)
        heavy_gp = sb("heavy_gp", [P, 2 * HG], I32)
        heavy_cols = sb("heavy_cols", [P, 2, 32], F32)
        heavy_none = sb("heavy_none", [P, 2, 32], F32)
        agg = sb("agg", [P, NT, C], F32)
        buf_a = sb("buf_a", [P, RING_A, 2, C], F32)
        buf_b = sb("buf_b", [P, RING_B, NT - 2, C], F32)
        agg_in = sb("agg_in", [P, RING_AGG, QT, C], F32)
        h_tile = sb("h_tile", [P, 2, C], F32)
        joined_t = sb("joined_t", [P, 2, KC * P], F32)

        turned_ps = [ps(f"turned_ps{i}", [P, KC * P]) for i in range(2)]
        y_ps = [ps(f"y_ps{i}", [P, OUT]) for i in range(2)]
        before_ps = ps("before_ps", [P, NV * NT])
        total_ps = ps("total_ps", [P, NV * NT])
        ranked_ps = ps("ranked_ps", [P, NT * COLS])

        const_landed = sem("const_landed")
        const_pool = sem("const_pool")
        const_dve = sem("const_dve")
        x_landed = [sem(f"x_landed{i}") for i in range(NQ)]
        adj_landed = [sem(f"adj_landed{i}") for i in range(RING_ADJ)]
        signed = sem("signed")
        pack_step = sem("pack_step")
        signs_used = sem("signs_used")
        bits_packed = sem("bits_packed")
        bits_stored = sem("bits_stored")
        found_ready = sem("found_ready")
        found_step = sem("found_step")
        onehot_ready = sem("onehot_ready")
        hist_ready = sem("hist_ready")
        select_ready = sem("select_ready")
        carried_step = sem("carried_step")
        ranked_ready = sem("ranked_ready")
        norm_step = sem("norm_step")
        stats_ready = sem("stats_ready")
        std_ready = sem("std_ready")
        norm_ready = sem("norm_ready")
        h_written = sem("h_written")
        h_stored = [sem(f"h_stored{i}") for i in range(2)]
        heavy_landed = sem("heavy_landed")
        heavy_step = sem("heavy_step")
        idx_ready = sem("idx_ready")
        bufs_zeroed = sem("bufs_zeroed")
        agg_zeroed = sem("agg_zeroed")
        gathered_first = sem("gathered_first")
        gathered = [sem(f"gathered{i}") for i in range(RING_A)]
        slot_maxed = sem("slot_maxed")
        group_step = sem("group_step")
        rest_maxed = sem("rest_maxed")
        scattered = [sem(f"scattered{i}") for i in range(NQ)]
        agg_landed = [sem(f"agg_landed{i}") for i in range(NQ)]
        h_ready = sem("h_ready")
        turned = sem("turned")
        joined = sem("joined")
        y_ready = sem("y_ready")
        y_copied = sem("y_copied")
        y_added = sem("y_added")
        out_stored = [sem(f"out_stored{i}") for i in range(NQ)]
        passed_pool, passed_dve, passed_act, passed_pe = [sem(f"passed_{e}") for e in ("pool", "dve", "act", "pe")]

        block = ctx.enter_context(nc.Block())

        @block.sync
        def _(sp):
            sp.dma_start(w_sb[:, :, :], w.rearrange("(k p) n -> p k n", p=P)).then_inc(const_landed, 16)
            sp.dma_start(b_sb[:, :], b.rearrange("(a n) -> a n", a=1)).then_inc(const_landed, 16)

            def load_x(nb, par, q):
                if due(level := value(nb, 16, -16)):
                    sp.wait_ge(out_stored[q], level)
                sp.dma_start(xs[:, par, q * QT:(q + 1) * QT, :],
                             x_rows[nb, :, q * QT:(q + 1) * QT, :]).then_inc(x_landed[q], 16)

            def load_adj(nb, t0, t1):
                for t in range(t0, t1):
                    if due(level := value(nb, NT, user_before(t, RING_ADJ, NT) + 1)):
                        sp.wait_ge(signed, level)
                    sp.dma_start(adj_in[:, t % RING_ADJ, :], adj_rows[nb, t]).then_inc(adj_landed[t % RING_ADJ], 16)

            def iteration(i, par, with_next=True):
                if with_next:
                    load_adj(i + 2, 0, 8)
                load_x(i + 1, 1 - par, 0)
                if with_next:
                    load_adj(i + 2, 8, 9)
                load_x(i + 1, 1 - par, 1)
                if with_next:
                    load_adj(i + 2, 9, 11)
                load_x(i + 1, 1 - par, 2)
                if with_next:
                    load_adj(i + 2, 11, 12)
                load_x(i + 1, 1 - par, 3)
                if with_next:
                    load_adj(i + 2, 12, NT)

            load_adj(0, 0, NT)
            for q in range(NQ):
                load_x(0, 0, q)
            load_adj(1, 0, NT)
            for q in range(NQ):
                load_x(1, 1, q)
            load_adj(2, 0, NT)
            with sp.Fori(0, B // 2 - 2) as pair:
                iteration(pair * 2 + 1, 1)
                iteration(pair * 2 + 2, 0)
            iteration(B - 3, 1)
            iteration(B - 2, 0, with_next=False)
            sp.wait_ge(bits_stored, B * 16)
            for s in out_stored:
                sp.wait_ge(s, B * 16)
            for s in h_stored:
                sp.wait_ge(s, B * 16 * NQ)
            for s in scattered:
                sp.wait_ge(s, B * 16 * QT)

        @block.gpsimd
        def _(pool):
            g = nc.gpsimd
            g.iota(iota_i[:, :], pattern=[[1, P]], base=0, channel_multiplier=0).then_inc(const_pool, 1)
            g.iota(position[:, :], pattern=[[1, N]], base=0, channel_multiplier=0).then_inc(const_pool, 1)
            g.iota(row_in_tile[:, :], pattern=[[0, 1]], base=0, channel_multiplier=1,
                   allow_small_or_imprecise_dtypes=True).then_inc(const_pool, 1)
            g.memset(ident[:, :], 0.0).then_inc(const_pool, 1)
            g.memset(before[:, :], 0.0).then_inc(const_pool, 1)
            pool.wait_ge(const_pool, 5)
            g.affine_select(out=ident[:, :], in_=ident[:, :], compare_op=ALU.not_equal, fill=1.0, base=0,
                            pattern=[[-1, P]], channel_multiplier=1).then_inc(const_pool, 1)
            g.affine_select(out=before[:, :], in_=before[:, :], compare_op=ALU.is_ge, fill=1.0, base=0,
                            pattern=[[-1, P]], channel_multiplier=1).then_inc(const_pool, 1)

            def gather(dst, par, column, s):
                pool.indirect_dma_start(dst, None, h_dram[par], bass.IndirectOffsetOnAxis(ap=column, axis=0),
                                        bounds_check=N - 1, oob_is_err=False).then_inc(s, 16)

            def past_two(n, one):
                one(2)
                with pool.If(n > 3):
                    one(3)
                with pool.If(n > 4):
                    one(4)
                    for t in range(5, 8):
                        with pool.If(n > t):
                            one(t)
                    with pool.If(n > 8):
                        one(8)
                        for t in range(9, NT):
                            with pool.If(n > t):
                                one(t)
                        pool.sem_inc(passed_pool, 1)
                    pool.sem_inc(passed_pool, 1)

            def heavy(i, par):
                pool.wait_ge(ranked_ready, value(i, 1, 1))
                pool.sem_inc(passed_pool, 1)
                pool.wait_ge(bits_stored, value(i, 16, 16))
                pool.sem_inc(passed_pool, 1)
                n = pool.value_load(n_tiles[0:1, par, S:S + 1], min_val=0, max_val=NT // 2)
                with pool.If(n > 0):
                    for t in range(NT):
                        with pool.If(n > t // 2):
                            pool.indirect_dma_start(
                                heavy_bits[:, t, :], None, bits_dram,
                                bass.IndirectOffsetOnAxis(ap=perm[:, par, t:t + 1], axis=0),
                                bounds_check=N - 1, oob_is_err=False).then_inc(heavy_landed, 16)
                    pool.sem_inc(passed_pool, 1)

            def scatter(b_, par):
                pool.wait_ge(slot_maxed, value(b_, NSLOT, NSLOT))
                pool.sem_inc(passed_pool, 1)
                pool.wait_ge(turned, value(b_, NT, CREDIT - NT))
                pool.sem_inc(passed_pool, 1)
                for t in range(NT):
                    pool.indirect_dma_start(
                        agg_dram[par], bass.IndirectOffsetOnAxis(ap=perm[:, par, t:t + 1], axis=0),
                        agg[:, t, :], None, bounds_check=N - 1, oob_is_err=False,
                    ).then_inc(scattered[t // QT], 16)

            def first_slot(i, par):
                n = pool.value_load(n_tiles[0:1, par, S - 1:S], min_val=0, max_val=NT)
                pairs = pool.value_load(n_tiles[0:1, par, S:S + 1], min_val=0, max_val=NT // 2)

                def one(t):
                    gather(agg[:, t, :], par, idx[:, par, 0, t:t + 1], gathered_first)

                for t in range(NT):
                    if t % QT == 0:
                        pool.wait_ge(agg_zeroed, value(i, NQ, t // QT + 1))
                        pool.sem_inc(passed_pool, 1)
                    with pool.If(pairs <= t // 2):
                        with pool.If(n > t):
                            one(t)
                        pool.sem_inc(passed_pool, 1)
                pool.wait_ge(idx_ready, value(i, 1, 1))
                pool.sem_inc(passed_pool, 1)
                for t in range(NT):
                    with pool.If(pairs > t // 2):
                        with pool.If(n > t):
                            one(t)
                        pool.sem_inc(passed_pool, 1)

            def one_slot(i, par, k):
                n = pool.value_load(n_tiles[0:1, par, S - 1 - k:S - k], min_val=0, max_val=NT)
                r = (k - 1) % RING_A

                def one(t):
                    dst = buf_a[:, r, t, :] if t < 2 else buf_b[:, k % RING_B, t - 2, :]
                    gather(dst, par, idx[:, par, k, t:t + 1], gathered[r])

                with pool.If(n > 0):
                    one(0)
                    with pool.If(n > 1):
                        one(1)
                    with pool.If(n > 2):
                        if k > RING_B:
                            pool.wait_ge(slot_maxed, value(i, NSLOT, k - RING_B))
                            pool.sem_inc(passed_pool, 1)
                        past_two(n, one)
                    pool.sem_inc(passed_pool, 1)

            def four_slots(i, par, g):
                k0 = SINGLE + 1 + 4 * g
                n = pool.value_load(n_tiles[0:1, par, S - 1 - k0:S - k0], min_val=0, max_val=NT)

                def four(t):
                    for k in range(k0, k0 + 4):
                        gather(buf_a[:, (k - 1) % RING_A, t, :], par, idx[:, par, k, t:t + 1],
                               gathered[(k - 1) % RING_A])

                with pool.If(n > 0):
                    pool.wait_ge(slot_maxed, value(i, NSLOT, k0 + 3 - RING_A))
                    pool.sem_inc(passed_pool, 1)
                    four(0)
                    with pool.If(n > 1):
                        four(1)
                    with pool.If(n > 2):
                        for k in range(k0, k0 + 4):
                            if k - RING_B < k0:
                                pool.wait_ge(slot_maxed, value(i, NSLOT, min(k - RING_B, k0 - 1)))
                            else:
                                pool.wait_ge(rest_maxed, pool.snap(rest_done, min_val=0, max_val=60000) + (k - RING_B - k0 + 1))
                            pool.sem_inc(passed_pool, 1)
                            past_two(n, lambda t: gather(buf_b[:, k % RING_B, t - 2, :], par, idx[:, par, k, t:t + 1],
                                                         gathered[(k - 1) % RING_A]))
                        pool.reg_add(rest_done, rest_done, 4)
                    pool.sem_inc(passed_pool, 1)

            def iteration(i, par, with_next=True):
                pool.wait_ge(ranked_ready, value(i, 1, 1))
                pool.sem_inc(passed_pool, 1)
                for s in h_stored:
                    pool.wait_ge(s, value(i, 16 * NQ, 16 * NQ))
                    pool.sem_inc(passed_pool, 1)
                first_slot(i, par)
                pool.wait_ge(bufs_zeroed, value(i, 1, 1))
                pool.sem_inc(passed_pool, 1)
                for k in range(1, SINGLE + 1):
                    one_slot(i, par, k)
                for g4 in range(NGRP):
                    four_slots(i, par, g4)
                if with_next:
                    heavy(i + 1, 1 - par)
                scatter(i, par)

            rest_done = pool.alloc_register("rest_done")
            pool.reg_mov(rest_done, 0)
            heavy(0, 0)
            iteration(0, 0)
            with pool.Fori(0, B // 2 - 1) as pair:
                iteration(pair * 2 + 1, 1)
                iteration(pair * 2 + 2, 0)
            iteration(B - 1, 1, with_next=False)

        @block.scalar
        def _(act):
            a = nc.scalar
            act.wait_ge(const_dve, 10)
            act.wait_ge(const_landed, 32)

            def zero_bufs(i):
                if due(level := value(i, NSLOT, 0)):
                    act.wait_ge(slot_maxed, level)
                    act.sem_inc(passed_act, 1)
                zb = zeros[:, :].unsqueeze(1)
                a.activation(buf_a[:, :, :, :].rearrange("p r t c -> p (r t) c"),
                             zb.to_broadcast([P, RING_A * 2, C]), ACT.Copy)
                a.activation(buf_b[:, :, :, :].rearrange("p r t c -> p (r t) c"),
                             zb.to_broadcast([P, RING_B * (NT - 2), C]), ACT.Copy).then_inc(bufs_zeroed, 1)

            def zero_agg(i):
                for q in range(NQ):
                    if due(level := value(i, 16 * QT, 0)):
                        act.wait_ge(scattered[q], level)
                    a.activation(agg[:, q * QT:(q + 1) * QT, :],
                                 zeros[:, :].unsqueeze(1).to_broadcast([P, QT, C]),
                                 ACT.Copy).then_inc(agg_zeroed, 1)

            def sign_tile(nb, t):
                if t % QT == 0:
                    if due(level := value(nb, NQ, t // QT - 1)):
                        act.wait_ge(signs_used, level)
                        act.sem_inc(passed_act, 1)
                act.wait_ge(adj_landed[t % RING_ADJ],
                            value(nb, 16 * len(range(t % RING_ADJ, NT, RING_ADJ)), 16 * (t // RING_ADJ) + 16))
                a.activation(
                    signs[:, t // QT % 2, t % QT, :].rearrange("p (w j e) -> p w e j", j=8, e=4),
                    adj_in[:, t % RING_ADJ, :].rearrange("p (w e j) -> p w e j", e=4, j=8),
                    ACT.Sign).then_inc(signed, 1)

            def store_bits(nb):
                act.wait_ge(bits_packed, value(nb, NQ, NQ))
                act.sem_inc(passed_act, 1)
                if due(level := value(nb, 1, 0)):
                    act.wait_ge(idx_ready, level)
                    act.sem_inc(passed_act, 1)
                act.dma_start(bits_rows, bits[:, :, :]).then_inc(bits_stored, 16)

            def norm(nb, par, half):
                t0, t1 = half * NT // 2, (half + 1) * NT // 2
                act.wait_ge(stats_ready, value(nb, 2, half + 1))
                a.activation(std[:, t0:t1], mean_var[:, t0:t1, 1], ACT.Sqrt, bias=eps[:, :]).then_inc(std_ready, 1)
                if due(level := value(nb, NSLOT, -NSLOT)):
                    act.wait_ge(slot_maxed, level)
                    act.sem_inc(passed_act, 1)
                act.wait_ge(norm_ready, value(nb, 2, half + 1))
                act.sem_inc(passed_act, 1)
                for pair_t in range(t0 // 2, t1 // 2):
                    if due(level := value(nb, 16 * NQ, 16 * (pair_t // 2))):
                        act.wait_ge(h_stored[pair_t % 2], level)
                        act.sem_inc(passed_act, 1)
                    for t in range(2 * pair_t, 2 * pair_t + 2):
                        a.activation(h_out[:, pair_t % 2, t % 2, :], xs[:, par, t, :], ACT.Relu,
                                     bias=shift[:, par, t:t + 1], scale=rstd[:, par, t:t + 1]).then_inc(h_written, 1)
                    act.wait_ge(h_written, value(nb, NT, 2 * pair_t + 2))
                    act.sem_inc(passed_act, 1)
                    act.dma_start(h_rows[par][:, 2 * pair_t:2 * pair_t + 2, :],
                                  h_out[:, pair_t % 2, :, :]).then_inc(h_stored[pair_t % 2], 16)

            def load_agg(b_, par, q):
                if q == 0:
                    for s in scattered:
                        act.wait_ge(s, value(b_, 16 * QT, 16 * QT))
                        act.sem_inc(passed_act, 1)
                act.wait_ge(y_added, value(b_, NQ, user_before(q, RING_AGG, NQ) + 1 + CREDIT))
                act.sem_inc(passed_act, 1)
                act.dma_start(agg_in[:, q % RING_AGG, :, :], agg_rows[par][:, q * QT:(q + 1) * QT, :]).then_inc(agg_landed[q], 16)

            def h_again(b_, par, t):
                act.wait_ge(turned, value(b_, NT, t - 1 + CREDIT))
                a.activation(h_tile[:, t % 2, :], xs[:, par, t, :], ACT.Relu, bias=shift[:, par, t:t + 1],
                             scale=rstd[:, par, t:t + 1]).then_inc(h_ready, 1)

            def join(b_, t):
                act.wait_ge(y_ready, value(b_, NT, t - 1 + CREDIT))
                act.wait_ge(turned, value(b_, NT, t + 1 + CREDIT))
                act.sem_inc(passed_act, 1)
                a.activation(joined_t[:, t % 2, :], turned_ps[t % 2][:, :], ACT.Copy).then_inc(joined, 1)

            def relu_y(b_, t):
                act.wait_ge(y_ready, value(b_, NT, t + 1 + CREDIT))
                a.activation(agg_in[:, t // QT % RING_AGG, t % QT, :], y_ps[t % 2][:, :], ACT.Relu).then_inc(y_copied, 1)

            def store_out(b_, par, q):
                act.wait_ge(y_added, value(b_, NQ, q + 1 + CREDIT))
                act.sem_inc(passed_act, 1)
                act.dma_start(out_rows[b_, :, q * QT:(q + 1) * QT, :],
                              xs[:, par, q * QT:(q + 1) * QT, :]).then_inc(out_stored[q], 16)

            def quad_c(b_, par, q, sign_of=None, sign_t=0):
                if 0 < q < NQ - 1:
                    load_agg(b_, par, q + 1)
                h_again(b_, par, q * QT)
                for t in range(q * QT, (q + 1) * QT):
                    if t + 1 < (q + 1) * QT:
                        h_again(b_, par, t + 1)
                    join(b_, t)
                    if sign_of is not None:
                        sign_tile(sign_of, sign_t + t % QT)
                    if t > q * QT:
                        relu_y(b_, t - 1)
                relu_y(b_, t)

            def iteration(i, par, with_a=True, with_next=True, with_b=True, with_c=True):
                other = 1 - par
                with_next = with_a and with_next
                if with_b:
                    zero_bufs(i)
                    zero_agg(i)
                if with_c:
                    load_agg(i - 1, other, 0)
                    load_agg(i - 1, other, 1)
                    quad_c(i - 1, other, 0)
                    quad_c(i - 1, other, 1, i + 2 if with_next else None, 0)
                    store_out(i - 1, other, 0)
                if with_a:
                    store_bits(i + 1)
                if with_c:
                    quad_c(i - 1, other, 2, i + 2 if with_next else None, 4)
                    store_out(i - 1, other, 1)
                    quad_c(i - 1, other, 3)
                    store_out(i - 1, other, 2)
                    if with_next:
                        for t in range(8, 12):
                            sign_tile(i + 2, t)
                if with_a:
                    norm(i + 1, other, 0)
                if with_c:
                    store_out(i - 1, other, 3)
                if with_a:
                    norm(i + 1, other, 1)
                if with_c and with_next:
                    for t in range(12, NT):
                        sign_tile(i + 2, t)
                if not with_c and with_next:
                    for t in range(NT):
                        sign_tile(i + 2, t)

            act.sem_inc(joined, CREDIT)
            act.sem_inc(y_copied, CREDIT)
            for t in range(NT):
                sign_tile(0, t)
            iteration(-1, 1, with_b=False, with_c=False)
            iteration(0, 0, with_c=False)
            with act.Fori(0, B // 2 - 2) as pair:
                iteration(pair * 2 + 1, 1)
                iteration(pair * 2 + 2, 0)
            iteration(B - 3, 1)
            iteration(B - 2, 0, with_next=False)
            iteration(B - 1, 1, with_a=False)
            iteration(B, 0, with_a=False, with_b=False)

        @block.tensor
        def _(pe):
            pe.wait_ge(const_pool, 7)
            pe.wait_ge(const_dve, 10)
            pe.wait_ge(const_landed, 32)

            def turn(b_, t):
                pe.wait_ge(joined, value(b_, NT, t - 1 + CREDIT))
                pe.wait_ge(h_ready, value(b_, NT, t + 1))
                pe.sem_inc(passed_pe, 1)
                if t % QT == 0:
                    pe.wait_ge(agg_landed[t // QT], value(b_, 16, 16))
                    pe.sem_inc(passed_pe, 1)
                for c in range(KC):
                    src = h_tile[:, t % 2, c * P:(c + 1) * P] if c < 2 else agg_in[:, t // QT % RING_AGG, t % QT, (c - 2) * P:(c - 1) * P]
                    last = nc.tensor.transpose(turned_ps[t % 2][:, c * P:(c + 1) * P], src, ident[:, :])
                last.then_inc(turned, 1)

            def multiply(b_, t):
                pe.wait_ge(y_copied, value(b_, NT, t - 1 + CREDIT))
                pe.wait_ge(joined, value(b_, NT, t + 1 + CREDIT))
                pe.sem_inc(passed_pe, 1)
                nc.tensor.matmul(y_ps[t % 2][:, :], ones_f[0:1, 0:P], b_sb[:, :], start=True, stop=False)
                for c in range(KC):
                    last = nc.tensor.matmul(y_ps[t % 2][:, :], joined_t[:, t % 2, c * P:(c + 1) * P], w_sb[:, c, :],
                                            start=False, stop=(c == KC - 1))
                last.then_inc(y_ready, 1)

            def products(b_, q):
                for t in range(q * QT, (q + 1) * QT):
                    turn(b_, t)
                    if t % QT:
                        multiply(b_, t - 1)
                multiply(b_, t)

            def histogram(nb):
                pe.wait_ge(onehot_ready, value(nb, 1, 1))
                flat = onehot[:, :, :].rearrange("p v t -> p (v t)")
                nc.tensor.matmul(before_ps[:, :], before[:, :], flat, start=True, stop=True)
                nc.tensor.matmul(total_ps[:, :], ones_bf[:, :], flat, start=True, stop=True).then_inc(hist_ready, 1)

            def carry(nb):
                for s in range(NT):
                    pe.wait_ge(select_ready, value(nb, NT, s + 1))
                    for d in range(NT):
                        last = nc.tensor.matmul(
                            ranked_ps[:, d * COLS:(d + 1) * COLS], select[:, s % 2, d * P:(d + 1) * P],
                            carried[:, s, :], start=(s == 0 and d == 0), stop=(s == NT - 1), skip_group_check=True)
                    last.then_inc(carried_step, 1)

            pe.sem_inc(turned, CREDIT)
            pe.sem_inc(y_ready, CREDIT)
            def iteration(i, with_a=True):
                products(i - 1, 0)
                products(i - 1, 1)
                if with_a:
                    histogram(i + 1)
                products(i - 1, 2)
                if with_a:
                    carry(i + 1)
                products(i - 1, 3)

            histogram(0)
            carry(0)
            histogram(1)
            carry(1)
            with pe.Fori(0, B // 2 - 1) as pair:
                iteration(pair * 2 + 1)
                iteration(pair * 2 + 2)
            iteration(B - 1, with_a=False)
            iteration(B, with_a=False)

        @block.vector
        def _(dve):
            v = nc.vector
            total_first = dve.alloc_register("total_first")
            totals = [dve.alloc_register(f"total{i}") for i in range(RING_A)]
            rest_done = dve.alloc_register("rest_done")
            heavy_total = dve.alloc_register("heavy_total")
            heavy_done = dve.alloc_register("heavy_done")
            for r in (total_first, *totals, rest_done, heavy_total, heavy_done):
                dve.reg_mov(r, 0)

            def read(r):
                return dve.snap(r, min_val=0, max_val=60000)

            v.memset(zeros[:, :], 0.0)
            v.memset(ones_f[:, :], 1.0)
            v.memset(ones_bf[:, :], 1.0)
            v.memset(eps[:, :], EPS)
            for i in range(GROUP):
                v.memset(bit_of[:, i:i + 1], 1 << i)
                v.memset(pick[:, i:i + 1], (1 << (7 + i)) | 127)
                v.memset(bit_late[:, i:i + 1], float(GROUP - i))
            for t in range(NT):
                ins = v.memset(tile_no[:, t:t + 1], float(t))
            ins.then_inc(const_dve, 1)
            dve.wait_ge(const_pool, 7)
            v.tensor_copy(group_no[:, :], iota_i[:, :]).then_inc(const_dve, 1)
            dve.wait_ge(const_dve, 2)
            v.tensor_scalar(group_late[:, :], group_no[:, :], -65536.0, 65536.0 * (NG - 1), ALU.mult,
                            ALU.add).then_inc(const_dve, 1)
            v.tensor_scalar(counts_down[:, :], group_no[:, 0:NV], -1.0, float(S), ALU.mult,
                            ALU.add).then_inc(const_dve, 1)
            for t in range(NT):
                ins = v.tensor_copy(carried[:, t, 2 * LIGHT:2 * LIGHT + 1], row_in_tile[:, :])
            ins.then_inc(const_dve, 1)
            v.tensor_copy(carried[:, :, 2 * LIGHT + 1], tile_no[:, :]).then_inc(const_dve, 5)
            dve.sem_inc(y_added, CREDIT)

            PACK = 7

            def pack_quad(nb, q):
                def step(n):
                    return value(nb, PACK * NQ, PACK * q + n)
                s = signs[:, q % 2, :, :].rearrange("p t n -> p (t n)").bitcast(U32)
                dve.wait_ge(signed, value(nb, NT, (q + 1) * QT))
                v.tensor_scalar(s, s, 0x01010101, None, ALU.bitwise_and).then_inc(pack_step, 1)
                if due(level := value(nb, NQ, q)):
                    dve.wait_ge(found_ready, level)
                    dve.sem_inc(passed_dve, 1)
                dve.wait_ge(pack_step, step(1))
                two = s.rearrange("p (n two) -> p n two", two=2)
                v.scalar_tensor_tensor(half1, two[:, :, 1], 1, two[:, :, 0], ALU.logical_shift_left,
                                       ALU.bitwise_or).then_inc(pack_step, 1)
                dve.wait_ge(pack_step, step(2))
                dve.sem_inc(passed_dve, 1)
                dve.sem_inc(signs_used, 1)
                two = half1.rearrange("p (n two) -> p n two", two=2)
                v.scalar_tensor_tensor(half2, two[:, :, 1], 2, two[:, :, 0], ALU.logical_shift_left,
                                       ALU.bitwise_or).then_inc(pack_step, 1)
                if q == 0:
                    if due(level := value(nb, 16, 0)):
                        dve.wait_ge(bits_stored, level)
                dve.wait_ge(pack_step, step(3))
                two = half2.rearrange("p (n two) -> p n two", two=2)
                quad = bits[:, q * QT:(q + 1) * QT, :]
                v.scalar_tensor_tensor(quad.rearrange("p t w -> p (t w)"), two[:, :, 1], 4, two[:, :, 0],
                                       ALU.logical_shift_left, ALU.bitwise_or).then_inc(pack_step, 1)
                dve.wait_ge(pack_step, step(4))
                dve.sem_inc(passed_dve, 1)
                dve.sem_inc(bits_packed, 1)
                v.scalar_tensor_tensor(keys[:, :, :], quad.bitcast(U16), 128.0,
                                       group_no[:, :].unsqueeze(1).to_broadcast([P, QT, NG]),
                                       ALU.mult, ALU.add).then_inc(pack_step, 1)
                dve.wait_ge(pack_step, step(5))
                dve.sem_inc(passed_dve, 1)
                for t in range(QT):
                    ins = v.max(top_groups[:, t, :], keys[:, t, :])
                ins.then_inc(pack_step, 1)
                dve.wait_ge(pack_step, step(6))
                v.tensor_tensor(cand[:, :, :, :].rearrange("p t g i -> p (t g) i"),
                                top_groups[:, :, :].rearrange("p t g -> p (t g)").unsqueeze(2).to_broadcast([P, QT * 8, GROUP]),
                                pick[:, :].unsqueeze(1).to_broadcast([P, QT * 8, GROUP]),
                                ALU.bitwise_and).then_inc(pack_step, 1)
                dve.wait_ge(pack_step, step(7))
                dve.sem_inc(passed_dve, 1)
                for t in range(QT):
                    ins = v.max(found[:, q * QT + t, :], cand[:, t, :, :].rearrange("p g i -> p (g i)"))
                ins.then_inc(found_ready, 1)

            NORM = 6

            def norm_stats(nb, par, half):
                t0, t1 = half * NT // 2, (half + 1) * NT // 2
                for q in range(2 * half, 2 * half + 2):
                    dve.wait_ge(x_landed[q], value(nb, 16, 16))
                    dve.sem_inc(passed_dve, 1)
                for t in range(t0, t1):
                    ins = v.bn_stats(stats[:, t, :], xs[:, par, t, :])
                ins.then_inc(norm_step, 1)
                if due(level := value(nb, 2, half - 1)):
                    dve.wait_ge(std_ready, level)
                    dve.sem_inc(passed_dve, 1)
                dve.wait_ge(norm_step, value(nb, NORM, 3 * half + 1))
                dve.sem_inc(passed_dve, 1)
                for t in range(t0, t1):
                    ins = v.bn_aggr(mean_var[:, t, :], stats[:, t, :])
                ins.then_inc(stats_ready, 1)

            def norm_scale(nb, par, half):
                t0, t1 = half * NT // 2, (half + 1) * NT // 2
                if due(level := value(nb, NT, t1 - 2 * NT)):
                    dve.wait_ge(h_ready, level)
                    dve.sem_inc(passed_dve, 1)
                dve.wait_ge(std_ready, value(nb, 2, half + 1))
                v.reciprocal(rstd[:, par, t0:t1], std[:, t0:t1]).then_inc(norm_step, 1)
                dve.wait_ge(norm_step, value(nb, NORM, 3 * half + 2))
                v.scalar_tensor_tensor(shift[:, par, t0:t1], mean_var[:, t0:t1, 0], -1.0, rstd[:, par, t0:t1], ALU.mult,
                                       ALU.mult).then_inc(norm_step, 1)
                dve.wait_ge(norm_step, value(nb, NORM, 3 * half + 3))
                dve.sem_inc(norm_ready, 1)

            RANK = 34

            def count_rows(nb, steps):
                f2 = found[:, :, :].rearrange("p t k -> p (t k)")
                dve.wait_ge(found_ready, value(nb, NQ, NQ))
                v.tensor_copy(found_f[:, :], f2).then_inc(found_step, steps.up())
                dve.wait_ge(found_step, steps.now)
                v.tensor_scalar(found_f[:, :].bitcast(I32), found_f[:, :].bitcast(I32), 23, None,
                                     ALU.logical_shift_right).then_inc(found_step, steps.up())
                v.tensor_scalar(f2, f2, 127, None, ALU.bitwise_and).then_inc(found_step, steps.up())
                dve.wait_ge(found_step, steps.now)
                dve.sem_inc(passed_dve, 1)
                if due(level := value(nb, NT, 0)):
                    dve.wait_ge(carried_step, level)
                v.tensor_copy(carried[:, :, 0:LIGHT], found[:, :, :]).then_inc(found_step, steps.up())
                v.tensor_scalar(carried[:, :, LIGHT:2 * LIGHT],
                                     found_f[:, :].bitcast(I32).rearrange("p (t k) -> p t k", k=8),
                                     -133.0, 0.0, ALU.add, ALU.max).then_inc(found_step, steps.up())

                half = bits[:, :, :].rearrange("p t w -> p (t w)").bitcast(U16)
                pa, pb = pop_a, pop_b
                v.tensor_scalar(pa, half, 1, 0x5555, ALU.logical_shift_right, ALU.bitwise_and).then_inc(found_step, steps.up())
                dve.wait_ge(found_step, steps.now)
                v.tensor_tensor(pb, half, pa, ALU.subtract).then_inc(found_step, steps.up())
                dve.wait_ge(found_step, steps.now)
                v.tensor_scalar(pa, pb, 2, 0x3333, ALU.logical_shift_right, ALU.bitwise_and).then_inc(found_step, steps.up())
                dve.wait_ge(found_step, steps.now)
                v.tensor_scalar(pb, pb, 0x3333, None, ALU.bitwise_and).then_inc(found_step, steps.up())
                dve.wait_ge(found_step, steps.now)
                v.tensor_tensor(pa, pa, pb, ALU.add).then_inc(found_step, steps.up())
                pa2, pb2 = pa[:, 0:NT * NG // 2], pb[:, 0:NT * NG // 2]
                both = pa.rearrange("p (t h n) -> p t h n", t=NT, h=2)
                dve.wait_ge(found_step, steps.now)
                v.tensor_tensor(pb2.rearrange("p (t n) -> p t n", t=NT), both[:, :, 0, :], both[:, :, 1, :],
                                ALU.add).then_inc(found_step, steps.up())
                dve.wait_ge(found_step, steps.now)
                v.tensor_scalar(pa2, pb2, 4, 0x0F0F, ALU.logical_shift_right, ALU.bitwise_and).then_inc(found_step, steps.up())
                v.tensor_scalar(pb2, pb2, 0x0F0F, None, ALU.bitwise_and).then_inc(found_step, steps.up())
                dve.wait_ge(found_step, steps.now)
                v.tensor_tensor(pa2, pa2, pb2, ALU.add).then_inc(found_step, steps.up())
                dve.wait_ge(found_step, steps.now)
                n = NG // 2
                src, dst = pop_a, pop_b
                while n > 8:
                    sv = src[:, 0:NT * n].rearrange("p (t h n) -> p t h n", t=NT, h=2)
                    dv = dst[:, 0:NT * n // 2].rearrange("p (t n) -> p t n", t=NT)
                    v.tensor_tensor(dv, sv[:, :, 0, :], sv[:, :, 1, :], ALU.add).then_inc(found_step, steps.up())
                    dve.wait_ge(found_step, steps.now)
                    src, dst, n = dst, src, n // 2
                v.tensor_reduce(count[:, :], src[:, 0:NT * n].bitcast(U8).rearrange("p (t n) -> p t n", t=NT),
                                     AX_X, ALU.add).then_inc(found_step, steps.up())
                dve.wait_ge(found_step, steps.now)
                v.tensor_scalar(count[:, :], count[:, :], float(S), None, ALU.min).then_inc(found_step, steps.up())
                dve.wait_ge(found_step, steps.now)
                dve.sem_inc(passed_dve, 1)
                if due(level := value(nb, 1, 0)):
                    dve.wait_ge(hist_ready, level)
                v.tensor_tensor(onehot[:, :, :], count[:, :].unsqueeze(1).to_broadcast([P, NV, NT]),
                                counts_down[:, :].unsqueeze(2).to_broadcast([P, NV, NT]),
                                ALU.is_equal).then_inc(onehot_ready, 1)

            def rank_rows(nb, steps):
                dve.wait_ge(hist_ready, value(nb, 1, 1))
                v.tensor_tensor_scan(cum[:, :], ones_f[:, :], total_ps[:, :], 0.0, ALU.mult, ALU.add).then_inc(found_step, steps.up())
                dve.wait_ge(found_step, steps.now)
                v.tensor_tensor(spot[:, :], cum[:, :], total_ps[:, :], ALU.subtract).then_inc(found_step, steps.up())
                dve.wait_ge(found_step, steps.now)
                v.tensor_tensor(spot[:, :], spot[:, :], before_ps[:, :], ALU.add).then_inc(found_step, steps.up())
                dve.wait_ge(found_step, steps.now)
                v.tensor_tensor(spot[:, :], spot[:, :], onehot[:, :, :].rearrange("p v t -> p (v t)"), ALU.mult).then_inc(found_step, steps.up())
                dve.wait_ge(found_step, steps.now)
                v.tensor_reduce(rank[:, :], spot[:, :].rearrange("p (v t) -> p t v", v=NV), AX_X, ALU.add).then_inc(found_step, steps.up())
                dve.wait_ge(found_step, steps.now)
                dve.sem_inc(passed_dve, 1)

            def select_rows(nb, s0, s1):
                for s in range(s0, s1):
                    if due(level := value(nb, NT, s - 1)):
                        dve.wait_ge(carried_step, level)
                    v.tensor_scalar(select[:, s % 2, :], position[:, :], rank[:, s:s + 1], None,
                                    ALU.is_equal).then_inc(select_ready, 1)

            def index_rows(nb, par, steps):
                for s in scattered:
                    if due(level := value(nb, 16 * QT, -16 * QT)):
                        dve.wait_ge(s, level)
                more_than = cum[:, :].rearrange("p (v t) -> p v t", v=NV)
                v.tensor_scalar(tiles_f[:, 0:S], more_than[:, 0:S, NT - 1], float(P - 1), None,
                                ALU.add).then_inc(found_step, steps.up())
                v.tensor_scalar(tiles_f[:, S:S + 1], more_than[:, S - 1 - LIGHT:S - LIGHT, NT - 1], float(2 * P - 1), None,
                                ALU.add).then_inc(found_step, steps.up())
                dve.wait_ge(found_step, steps.now)
                v.tensor_scalar(n_tiles[:, par, 0:S], tiles_f[:, 0:S], 7, None,
                                ALU.logical_shift_right).then_inc(found_step, steps.up())
                v.tensor_scalar(n_tiles[:, par, S:S + 1], tiles_f[:, S:S + 1], 8, None,
                                ALU.logical_shift_right).then_inc(found_step, steps.up())
                dve.wait_ge(carried_step, value(nb, NT, NT))
                v.tensor_copy(ranked[:, :, :].rearrange("p t c -> p (t c)"), ranked_ps[:, :]).then_inc(found_step, steps.up())
                dve.wait_ge(found_step, steps.now)
                dve.sem_inc(passed_dve, 1)
                group, bit1 = ranked[:, :, 0:LIGHT], ranked[:, :, LIGHT:2 * LIGHT]
                so = slot_of[:, :].rearrange("p (t k) -> p t k", k=8)
                no = no_slot[:, :].rearrange("p (t k) -> p t k", k=8)
                v.scalar_tensor_tensor(so, group, float(GROUP), bit1, ALU.mult, ALU.add).then_inc(found_step, steps.up())
                v.tensor_scalar(no, bit1, 0.0, float(SKIP), ALU.is_equal, ALU.mult).then_inc(found_step, steps.up())
                v.scalar_tensor_tensor(row_of[:, :], ranked[:, :, 2 * LIGHT + 1], float(P),
                                            ranked[:, :, 2 * LIGHT], ALU.mult, ALU.add).then_inc(found_step, steps.up())
                dve.wait_ge(found_step, steps.now)
                v.scalar_tensor_tensor(idx[:, par, 0:LIGHT, :].rearrange("p k t -> p t k"), so, -1.0, no,
                                            ALU.add, ALU.add).then_inc(found_step, steps.up())
                v.tensor_copy(perm[:, par, :], row_of[:, :]).then_inc(found_step, steps.up())
                dve.wait_ge(found_step, steps.now)
                dve.sem_inc(passed_dve, 1)
                dve.sem_inc(ranked_ready, 1)
                assert steps.n == RANK, steps.n

            HEAVY = 37

            def heavy_pair(par, d):
                steps = Steps(read(heavy_done))
                half = heavy_bits[:, bass.ds(d * 2, 2), :].rearrange("p t w -> p (t w)").bitcast(U16)
                key = heavy_key[:, :, :].rearrange("p t g -> p (t g)")
                late = group_late[:, :].unsqueeze(1).to_broadcast([P, 2, NG])
                v.scalar_tensor_tensor(heavy_key[:, :, :], half.rearrange("p (t g) -> p t g", t=2), 0.0, late, ALU.is_gt,
                                       ALU.mult).then_inc(heavy_step, steps.up())
                dve.wait_ge(heavy_step, steps.now)
                v.tensor_tensor(key, key, half, ALU.add).then_inc(heavy_step, steps.up())
                dve.wait_ge(heavy_step, steps.now)
                dve.sem_inc(passed_dve, 1)
                for r in range(4):
                    eights = [heavy_groups[:, t, 8 * r:8 * r + 8] for t in range(2)]
                    for t in range(2):
                        if r:
                            dve.wait_ge(heavy_step, steps.now - 1)
                            dve.sem_inc(passed_dve, 1)
                        v.max(eights[t], heavy_key[:, t, :]).then_inc(heavy_step, steps.up())
                    if r < 3:
                        for t in range(2):
                            dve.wait_ge(heavy_step, steps.now - 1)
                            dve.sem_inc(passed_dve, 1)
                            v.match_replace(heavy_key[:, t, :], eights[t], heavy_key[:, t, :],
                                            0.0).then_inc(heavy_step, steps.up())
                dve.wait_ge(heavy_step, steps.now)
                v.tensor_copy(heavy_gi[:, :].rearrange("p (t g) -> p t g", t=2), heavy_groups[:, :, 0:HG]).then_inc(heavy_step, steps.up())
                dve.wait_ge(heavy_step, steps.now)
                v.tensor_scalar(heavy_gp[:, :], heavy_gi[:, :], 16, 4, ALU.logical_shift_right,
                                ALU.logical_shift_left).then_inc(heavy_step, steps.up())
                v.tensor_tensor(heavy_bit[:, :, :], heavy_gi[:, :].unsqueeze(2).to_broadcast([P, 2 * HG, GROUP]),
                                bit_of[:, :].unsqueeze(1).to_broadcast([P, 2 * HG, GROUP]),
                                ALU.bitwise_and).then_inc(heavy_step, steps.up())
                dve.wait_ge(heavy_step, steps.now)
                v.tensor_tensor(heavy_pos[:, :, :], heavy_gp[:, :].unsqueeze(2).to_broadcast([P, 2 * HG, GROUP]),
                                bit_late[:, :].unsqueeze(1).to_broadcast([P, 2 * HG, GROUP]),
                                ALU.add).then_inc(heavy_step, steps.up())
                dve.wait_ge(heavy_step, steps.now)
                pos = heavy_pos[:, :, :].rearrange("p g i -> p (g i)")
                v.scalar_tensor_tensor(pos, heavy_bit[:, :, :].rearrange("p g i -> p (g i)"), 0.0, pos, ALU.is_gt,
                                       ALU.mult).then_inc(heavy_step, steps.up())
                dve.wait_ge(heavy_step, steps.now)
                dve.sem_inc(passed_dve, 1)
                of_tile = [pos[:, t * HG * GROUP:(t + 1) * HG * GROUP] for t in range(2)]
                for r in range(4):
                    eights = [heavy_cols[:, t, 8 * r:8 * r + 8] for t in range(2)]
                    for t in range(2):
                        if r:
                            dve.wait_ge(heavy_step, steps.now - 1)
                            dve.sem_inc(passed_dve, 1)
                        v.max(eights[t], of_tile[t]).then_inc(heavy_step, steps.up())
                    if r < 3:
                        for t in range(2):
                            dve.wait_ge(heavy_step, steps.now - 1)
                            dve.sem_inc(passed_dve, 1)
                            v.match_replace(of_tile[t], eights[t], of_tile[t], 0.0).then_inc(heavy_step, steps.up())
                dve.wait_ge(heavy_step, steps.now)
                v.tensor_scalar(heavy_none[:, :, :], heavy_cols[:, :, :], 0.0, float(SKIP), ALU.is_equal,
                                ALU.mult).then_inc(heavy_step, steps.up())
                dve.wait_ge(heavy_step, steps.now)
                v.scalar_tensor_tensor(idx[:, par, :, bass.ds(d * 2, 2)].rearrange("p k t -> p t k"),
                                       heavy_none[:, :, 0:S], float(N), heavy_cols[:, :, 0:S], ALU.add,
                                       ALU.subtract).then_inc(heavy_step, steps.up())
                assert steps.n == HEAVY, steps.n
                dve.reg_add(heavy_done, heavy_done, HEAVY)
                dve.wait_ge(heavy_step, read(heavy_done))
                dve.sem_inc(passed_dve, 1)

            def heavy_rows(i, par):
                n = dve.value_load(n_tiles[0:1, par, S:S + 1], min_val=0, max_val=NT // 2)
                dve.reg_add(heavy_total, heavy_total, n * 32)
                with dve.If(n > 0):
                    dve.wait_ge(heavy_landed, read(heavy_total))
                    dve.sem_inc(passed_dve, 1)
                    with dve.Fori(0, n) as d:
                        heavy_pair(par, d)
                    dve.sem_inc(passed_dve, 1)
                dve.sem_inc(idx_ready, 1)

            def maxed(lo, hi, k):
                src = buf_a[:, (k - 1) % RING_A, lo:hi, :] if hi <= 2 else buf_b[:, k % RING_B, lo - 2:hi - 2, :]
                dst = agg[:, lo:hi, :]
                return v.tensor_tensor(dst, dst, src, ALU.max)

            def slot(i, par, k):
                n = dve.value_load(n_tiles[0:1, par, S - 1 - k:S - k], min_val=0, max_val=NT)
                if k == 1:
                    n0 = dve.value_load(n_tiles[0:1, par, S - 1:S], min_val=0, max_val=NT)
                    dve.reg_add(total_first, total_first, n0 * 16)
                    dve.wait_ge(agg_zeroed, value(i, NQ, NQ))
                    dve.sem_inc(passed_dve, 1)
                    dve.wait_ge(bufs_zeroed, value(i, 1, 1))
                    dve.sem_inc(passed_dve, 1)
                    with dve.If(n0 > 0):
                        dve.wait_ge(gathered_first, read(total_first))
                        dve.sem_inc(passed_dve, 1)
                total = totals[(k - 1) % RING_A]
                dve.reg_add(total, total, n * 16)
                if due(level := value(i, NSLOT, k - 1)):
                    dve.wait_ge(slot_maxed, level)
                    dve.sem_inc(passed_dve, 1)
                with dve.If(n > 0):
                    dve.wait_ge(gathered[(k - 1) % RING_A], read(total))
                    dve.sem_inc(passed_dve, 1)
                    with dve.If(n > 1):
                        with dve.If(n > 2):
                            with dve.If(n > 4):
                                with dve.If(n > 8):
                                    maxed(8, NT, k)
                                maxed(4, 8, k)
                            maxed(2, 4, k)
                        maxed(1, 2, k)
                    dve.sem_inc(passed_dve, 1)
                maxed(0, 1, k).then_inc(slot_maxed, 1)

            def four_slots(i, par, g4):
                k0 = SINGLE + 1 + 4 * g4
                r = (k0 - 1) % RING_A
                n = dve.value_load(n_tiles[0:1, par, S - 1 - k0:S - k0], min_val=0, max_val=NT)
                dve.wait_ge(slot_maxed, value(i, NSLOT, k0 - 1))
                dve.sem_inc(passed_dve, 1)
                for j in range(4):
                    dve.reg_add(totals[r + j], totals[r + j], n * 16)
                with dve.If(n > 0):
                    with dve.If(n > 2):
                        for j in range(4):
                            dve.wait_ge(gathered[r + j], read(totals[r + j]))
                            dve.sem_inc(passed_dve, 1)
                            with dve.If(n > 4):
                                with dve.If(n > 8):
                                    maxed(8, NT, k0 + j)
                                maxed(4, 8, k0 + j)
                            maxed(2, 4, k0 + j).then_inc(rest_maxed, 1)
                            dve.reg_add(rest_done, rest_done, 1)
                            dve.wait_ge(rest_maxed, read(rest_done))
                            dve.sem_inc(passed_dve, 1)
                    for j in range(4):
                        dve.wait_ge(gathered[r + j], read(totals[r + j]))
                        dve.sem_inc(passed_dve, 1)

                def fold(t):
                    return v.tensor_tensor(buf_a[:, r:r + 2, t, :], buf_a[:, r:r + 2, t, :], buf_a[:, r + 2:r + 4, t, :],
                                           ALU.max)

                with dve.If(n > 1):
                    fold(1)
                fold(0).then_inc(group_step, 1)
                dve.wait_ge(group_step, value(i, 2 * NGRP, 2 * g4 + 1))
                dve.sem_inc(passed_dve, 1)
                with dve.If(n > 1):
                    maxed(1, 2, k0)
                maxed(0, 1, k0).then_inc(group_step, 1)
                dve.wait_ge(group_step, value(i, 2 * NGRP, 2 * g4 + 2))
                dve.sem_inc(passed_dve, 1)
                with dve.If(n > 1):
                    maxed(1, 2, k0 + 1)
                maxed(0, 1, k0 + 1).then_inc(slot_maxed, 4)

            def add_x(b_, par, q):
                dve.wait_ge(y_copied, value(b_, NT, (q + 1) * QT + CREDIT))
                quad = xs[:, par, q * QT:(q + 1) * QT, :]
                v.tensor_tensor(quad, quad, agg_in[:, q % RING_AGG, :, :], ALU.add).then_inc(y_added, 1)

            def iteration(i, par, with_a=True, with_next=True, with_b=True, with_c=True):
                nb, other = i + 1, 1 - par
                with_next = with_a and with_next
                steps = Steps(nb * RANK)
                if with_a:
                    pack_quad(nb, 2)
                    pack_quad(nb, 3)
                    if not with_c:
                        norm_stats(nb, other, 0)
                        norm_scale(nb, other, 0)
                        norm_stats(nb, other, 1)
                        norm_scale(nb, other, 1)
                if with_c:
                    add_x(i - 1, other, 0)
                if with_a:
                    count_rows(nb, steps)
                if with_b:
                    slot(i, par, 1)
                if with_c:
                    add_x(i - 1, other, 1)
                if with_a:
                    rank_rows(nb, steps)
                if with_b:
                    slot(i, par, 2)
                if with_a:
                    select_rows(nb, 0, NT // 2)
                if with_b:
                    slot(i, par, 3)
                if with_a:
                    select_rows(nb, NT // 2, NT)
                if with_c:
                    add_x(i - 1, other, 2)
                if with_b:
                    slot(i, par, 4)
                if with_next:
                    pack_quad(nb + 1, 0)
                if with_b:
                    slot(i, par, 5)
                if with_a:
                    index_rows(nb, other, steps)
                    if with_c:
                        norm_stats(nb, other, 0)
                if with_b:
                    slot(i, par, 6)
                if with_a and with_c:
                    norm_scale(nb, other, 0)
                if with_c:
                    add_x(i - 1, other, 3)
                if with_b:
                    slot(i, par, 7)
                    slot(i, par, 8)
                if with_next:
                    pack_quad(nb + 1, 1)
                if with_b:
                    four_slots(i, par, 0)
                if with_a and with_c:
                    norm_stats(nb, other, 1)
                if with_b:
                    four_slots(i, par, 1)
                if with_a and with_c:
                    norm_scale(nb, other, 1)
                if with_b:
                    four_slots(i, par, 2)
                    four_slots(i, par, 3)
                if with_a:
                    heavy_rows(nb, other)

            pack_quad(0, 0)
            pack_quad(0, 1)
            iteration(-1, 1, with_b=False, with_c=False)
            iteration(0, 0, with_c=False)
            with dve.Fori(0, B // 2 - 2) as pair:
                iteration(pair * 2 + 1, 1)
                iteration(pair * 2 + 2, 0)
            iteration(B - 3, 1)
            iteration(B - 2, 0, with_next=False)
            iteration(B - 1, 1, with_a=False)
            iteration(B, 0, with_a=False, with_b=False)


_INS = ["x", "adj", "L0_gnn_W", "L0_gnn_b"]


def kernel(**inputs):
    import numpy as _np
    import concourse.bacc as _bacc
    from concourse import mybir as _mybir
    from concourse.bass_utils import run_bass_kernel_spmd as _run

    nc = _bacc.Bacc("TRN2", target_bir_lowering=False, num_devices=1)
    arrays, args = {}, []
    for name in _INS:
        a = _np.ascontiguousarray(inputs[name])
        arrays[f"in_{name}_dram"] = a
        args.append(nc.dram_tensor(f"in_{name}_dram", a.shape, _mybir.dt.from_np(a.dtype), kind="ExternalInput").ap())
    shape = tuple(inputs["x"].shape)
    args.append(nc.dram_tensor("out_dram", shape, _mybir.dt.float32, kind="ExternalOutput").ap())
    build(nc, *args)
    r = _run(nc, [arrays], core_ids=[0])
    return r.results[0]["out_dram"]
```

```python
from contextlib import ExitStack

import concourse.bass as bass
from concourse import mybir

ALU = mybir.AluOpType
ACT = mybir.ActivationFunctionType
F32 = mybir.dt.float32
BF16 = mybir.dt.bfloat16
I32 = mybir.dt.int32
U32 = mybir.dt.uint32
I16 = mybir.dt.int16
U16 = mybir.dt.uint16
I8 = mybir.dt.int8
U8 = mybir.dt.uint8
AX_X = mybir.AxisListType.X

P = 128
S = 25
LIGHT = 8
GROUP = 16
QT = 4
RING_A, RING_B = 8, 2
SINGLE = 8
RING_ADJ, RING_AGG = 3, 3
SKIP = 1 << 20
CREDIT = 32
EPS = 1e-5


def value(batch, per_batch, more):
    return batch * per_batch + more


def due(level):
    return not isinstance(level, int) or level > 0


def user_before(n, ring, per_batch):
    return n - ring if n >= ring else range(n, per_batch, ring)[-1] - per_batch


class Steps:

    def __init__(self, base):
        self.base, self.n = base, 0

    def up(self):
        self.n += 1
        return 1

    @property
    def now(self):
        return self.base + self.n


def build(nc, x, adj, w, b, out):
    B, N, C = x.shape
    OUT = w.shape[1]
    NT = N // P
    NQ = NT // QT
    NG = N // GROUP
    WORDS = N // 32
    KC = 2 * C // P
    NV = S + 1
    NSLOT = S - 1
    NGRP = (NSLOT - SINGLE) // 4
    COLS = 2 * LIGHT + 2
    HALF = NT // 2
    HG = S
    assert NT == 16 and NG == P and C == OUT == 256 and KC == 4

    x_rows = x.rearrange("b (t p) c -> b p t c", p=P)
    out_rows = out.rearrange("b (t p) c -> b p t c", p=P)
    adj_rows = adj.rearrange("b (t p) j -> b t p j", p=P)
    h_dram = [nc.dram_tensor(f"h_table{i}", [N, C], F32).ap() for i in range(2)]
    agg_dram = [nc.dram_tensor(f"agg_table{i}", [N, C], F32).ap() for i in range(2)]
    bits_dram = nc.dram_tensor("bits_table", [N, WORDS], U32).ap()
    h_rows = [d.rearrange("(t p) c -> p t c", p=P) for d in h_dram]
    agg_rows = [d.rearrange("(t p) c -> p t c", p=P) for d in agg_dram]
    bits_rows = bits_dram.rearrange("(t p) j -> p t j", p=P)

    with ExitStack() as ctx:
        def sb(name, shape, dt):
            return ctx.enter_context(nc.sbuf_tensor(name, shape, dt))

        def ps(name, shape):
            return ctx.enter_context(nc.psum_tensor(name, shape, F32))

        def sem(name):
            return ctx.enter_context(nc.semaphore(name))

        ident = sb("ident", [P, P], F32)
        before = sb("before", [P, P], BF16)
        ones_bf = sb("ones_bf", [P, P], BF16)
        ones_f = sb("ones_f", [P, NV * NT], F32)
        zeros = sb("zeros", [P, C], F32)
        eps = sb("eps", [P, 1], F32)
        w_sb = sb("w_sb", [P, KC, OUT], F32)
        b_parts = sb("b_parts", [3, OUT], BF16)
        position = sb("position", [P, N], I16)
        group_no = sb("group_no", [P, NG], F32)
        group_late = sb("group_late", [P, NG], F32)
        bit_late = sb("bit_late", [P, GROUP], F32)
        bit_of = sb("bit_of", [P, GROUP], I32)
        pick = sb("pick", [P, GROUP], I32)
        counts_down = sb("counts_down", [P, NV], F32)
        iota_i = sb("iota_i", [P, P], I32)
        row_in_tile = sb("row_in_tile", [P, 1], F32)
        tile_no = sb("tile_no", [P, NT], F32)

        xs = sb("xs", [P, 2, NT, C], F32)
        adj_in = sb("adj_in", [P, RING_ADJ, N], I32)
        signs = sb("signs", [P, 2, QT, N], I8)
        work_a = sb("work_a", [P, QT * N // 8], U32)
        work_b = sb("work_b", [P, QT * N // 8], U32)
        half1 = work_a[:, :]
        half2 = work_b[:, 0:QT * N // 16]
        keys = work_b[:, QT * NG:2 * QT * NG].bitcast(I32).rearrange("p (t g) -> p t g", t=QT)
        cand = work_a[:, 0:QT * 8 * GROUP].bitcast(I32).rearrange("p (t g i) -> p t g i", t=QT, g=8)
        pop_a = work_a[:, :].bitcast(U16)
        pop_b = work_b[:, :].bitcast(U16)
        heavy_bit = work_a[:, 0:2 * HG * GROUP].bitcast(I32).rearrange("p (g i) -> p g i", i=GROUP)
        heavy_pos = work_b[:, 0:2 * HG * GROUP].bitcast(F32).rearrange("p (g i) -> p g i", i=GROUP)
        b_sb = work_a[0:3, 0:OUT].bitcast(F32)
        b_sum = work_a[0:3, OUT:2 * OUT].bitcast(F32)
        b_part = work_b[0:3, 0:3 * OUT // 2].bitcast(BF16).rearrange("p (k n) -> p k n", k=3)
        bits = sb("bits", [P, NT, WORDS], U32)
        top_groups = sb("top_groups", [P, QT, 8], I32)
        found = sb("found", [P, NT, 8], I32)
        found_f = sb("found_f", [P, NT * 8], F32)
        carried = sb("carried", [P, NT, COLS], BF16)
        count = sb("count", [P, NT], F32)
        onehot = sb("onehot", [P, NV, NT], BF16)
        cum = sb("cum", [P, NV * NT], F32)
        spot = sb("spot", [P, NV * NT], F32)
        rank = sb("rank", [P, NT], F32)
        select = sb("select", [P, 2, N], BF16)
        tiles_f = sb("tiles_f", [P, S + 1], I32)
        n_past_two = sb("n_past_two", [P, 2, S], I32)
        n_high = sb("n_high", [P, 2, 1], I32)
        n_tiles = sb("n_tiles", [P, 2, S + 1], I32)
        ranked = sb("ranked", [P, NT, COLS], F32)
        slot_of = sb("slot_of", [P, NT * 8], F32)
        no_slot = sb("no_slot", [P, NT * 8], F32)
        row_of = sb("row_of", [P, NT], F32)
        perm = sb("perm", [P, 2, NT], U32)
        idx = sb("idx", [P, 2, S, NT], U32)
        stats = sb("stats", [P, NT, 6], F32)
        mean_var = sb("mean_var", [P, NT, 2], F32)
        std = sb("std", [P, NT], F32)
        rstd = sb("rstd", [P, 2, NT], F32)
        shift = sb("shift", [P, 2, NT], F32)
        h_out = sb("h_out", [P, 2, 2, C], F32)
        heavy_bits = sb("heavy_bits", [P, NT, WORDS], U32)
        heavy_key = sb("heavy_key", [P, 2, NG], F32)
        heavy_groups = sb("heavy_groups", [P, 2, 32], F32)
        heavy_gi = sb("heavy_gi", [P, 2 * HG], I32)
        heavy_gp = sb("heavy_gp", [P, 2 * HG], I32)
        heavy_cols = sb("heavy_cols", [P, 2, 32], F32)
        heavy_none = sb("heavy_none", [P, 2, 32], F32)
        agg = sb("agg", [P, NT, C], F32)
        buf_a = sb("buf_a", [P, RING_A, 2, C], F32)
        buf_b = sb("buf_b", [P, RING_B, NT - 2, C], F32)
        agg_in = sb("agg_in", [P, RING_AGG, QT, C], F32)
        h_tile = sb("h_tile", [P, 2, C], F32)
        joined_t = sb("joined_t", [P, 2, KC * P], F32)

        turned_ps = [ps(f"turned_ps{i}", [P, KC * P]) for i in range(2)]
        y_ps = [ps(f"y_ps{i}", [P, OUT]) for i in range(2)]
        before_ps = ps("before_ps", [P, NV * NT])
        total_ps = ps("total_ps", [P, NV * NT])
        ranked_ps = ps("ranked_ps", [P, NT * COLS])

        const_landed = sem("const_landed")
        const_pool = sem("const_pool")
        const_dve = sem("const_dve")
        bias_step = sem("bias_step")
        x_landed = [sem(f"x_landed{i}") for i in range(NQ)]
        adj_landed = [sem(f"adj_landed{i}") for i in range(RING_ADJ)]
        signed = sem("signed")
        pack_step = sem("pack_step")
        signs_used = sem("signs_used")
        bits_packed = sem("bits_packed")
        bits_stored = sem("bits_stored")
        found_ready = sem("found_ready")
        found_step = sem("found_step")
        onehot_ready = sem("onehot_ready")
        hist_ready = sem("hist_ready")
        select_ready = sem("select_ready")
        carried_step = sem("carried_step")
        ranked_ready = sem("ranked_ready")
        norm_step = sem("norm_step")
        stats_ready = sem("stats_ready")
        std_ready = sem("std_ready")
        norm_ready = sem("norm_ready")
        h_written = sem("h_written")
        h_stored = [sem(f"h_stored{i}") for i in range(2)]
        heavy_landed = sem("heavy_landed")
        heavy_step = sem("heavy_step")
        idx_ready = sem("idx_ready")
        buf_a_zeroed = sem("buf_a_zeroed")
        buf_b_zeroed = sem("buf_b_zeroed")
        buf_b_free = sem("buf_b_free")
        gathered_first = sem("gathered_first")
        gathered_high = sem("gathered_high")
        gathered = [sem(f"gathered{i}") for i in range(RING_A)]
        gathered_tail = [[sem(f"gathered_tail{i}_{t}") for t in range(2)] for i in range(2)]
        low_maxed = sem("low_maxed")
        slot_maxed = sem("slot_maxed")
        group_step = sem("group_step")
        rest_maxed = sem("rest_maxed")
        scattered = [sem(f"scattered{i}") for i in range(NQ)]
        agg_landed = [sem(f"agg_landed{i}") for i in range(NQ)]
        h_ready = sem("h_ready")
        turned = sem("turned")
        joined = sem("joined")
        y_ready = sem("y_ready")
        y_copied = sem("y_copied")
        y_added = sem("y_added")
        out_stored = [sem(f"out_stored{i}") for i in range(NQ)]
        passed_pool, passed_dve, passed_act, passed_pe = [sem(f"passed_{e}") for e in ("pool", "dve", "act", "pe")]

        block = ctx.enter_context(nc.Block())

        @block.sync
        def _(sp):
            sp.dma_start(w_sb[:, :, :], w.rearrange("(k p) n -> p k n", p=P)).then_inc(const_landed, 16)
            for p in range(3):
                sp.dma_start(b_sb[p:p + 1, :], b.rearrange("(a n) -> a n", a=1)).then_inc(const_landed, 16)

            def load_x(nb, par, q):
                if due(level := value(nb, 16, -16)):
                    sp.wait_ge(out_stored[q], level)
                sp.dma_start(xs[:, par, q * QT:(q + 1) * QT, :],
                             x_rows[nb, :, q * QT:(q + 1) * QT, :]).then_inc(x_landed[q], 16)

            def load_adj(nb, t0, t1):
                for t in range(t0, t1):
                    if due(level := value(nb, NT, user_before(t, RING_ADJ, NT) + 1)):
                        sp.wait_ge(signed, level)
                    sp.dma_start(adj_in[:, t % RING_ADJ, :], adj_rows[nb, t]).then_inc(adj_landed[t % RING_ADJ], 16)

            def iteration(i, par, with_next=True):
                if with_next:
                    load_adj(i + 2, 0, NT)
                for q in range(NQ):
                    load_x(i + 1, 1 - par, q)

            load_adj(0, 0, NT)
            for q in range(NQ):
                load_x(0, 0, q)
            load_adj(1, 0, NT)
            for q in range(NQ):
                load_x(1, 1, q)
            load_adj(2, 0, NT)
            with sp.Fori(0, B // 2 - 2) as pair:
                iteration(pair * 2 + 1, 1)
                iteration(pair * 2 + 2, 0)
            iteration(B - 3, 1)
            iteration(B - 2, 0, with_next=False)
            sp.wait_ge(bits_stored, B * 16)
            for s in out_stored:
                sp.wait_ge(s, B * 16)
            for s in h_stored:
                sp.wait_ge(s, B * 16 * NQ)
            for s in scattered:
                sp.wait_ge(s, B * 16 * QT)

        @block.gpsimd
        def _(pool):
            g = nc.gpsimd
            g.iota(iota_i[:, :], pattern=[[1, P]], base=0, channel_multiplier=0).then_inc(const_pool, 1)
            g.iota(position[:, :], pattern=[[1, N]], base=0, channel_multiplier=0).then_inc(const_pool, 1)
            g.iota(row_in_tile[:, :], pattern=[[0, 1]], base=0, channel_multiplier=1,
                   allow_small_or_imprecise_dtypes=True).then_inc(const_pool, 1)
            g.memset(ident[:, :], 0.0).then_inc(const_pool, 1)
            g.memset(before[:, :], 0.0).then_inc(const_pool, 1)
            pool.wait_ge(const_pool, 5)
            g.affine_select(out=ident[:, :], in_=ident[:, :], compare_op=ALU.not_equal, fill=1.0, base=0,
                            pattern=[[-1, P]], channel_multiplier=1).then_inc(const_pool, 1)
            g.affine_select(out=before[:, :], in_=before[:, :], compare_op=ALU.is_ge, fill=1.0, base=0,
                            pattern=[[-1, P]], channel_multiplier=1).then_inc(const_pool, 1)

            def gather(dst, par, column, s):
                pool.indirect_dma_start(dst, None, h_dram[par], bass.IndirectOffsetOnAxis(ap=column, axis=0),
                                        bounds_check=N - 1, oob_is_err=False).then_inc(s, 16)

            def past_two(n, one):
                one(2)
                with pool.If(n > 3):
                    one(3)
                with pool.If(n > 4):
                    one(4)
                    for t in range(5, 8):
                        with pool.If(n > t):
                            one(t)
                    with pool.If(n > 8):
                        one(8)
                        for t in range(9, NT):
                            with pool.If(n > t):
                                one(t)
                        pool.sem_inc(passed_pool, 1)
                    pool.sem_inc(passed_pool, 1)

            def heavy(i, par):
                pool.wait_ge(ranked_ready, value(i, 1, 1))
                pool.sem_inc(passed_pool, 1)
                pool.wait_ge(bits_stored, value(i, 16, 16))
                pool.sem_inc(passed_pool, 1)
                n = pool.value_load(n_tiles[0:1, par, S:S + 1])
                with pool.If(n > 0):
                    for t in range(NT):
                        with pool.If(n > t // 2):
                            pool.indirect_dma_start(
                                heavy_bits[:, t, :], None, bits_dram,
                                bass.IndirectOffsetOnAxis(ap=perm[:, par, t:t + 1], axis=0),
                                bounds_check=N - 1, oob_is_err=False).then_inc(heavy_landed, 16)
                    pool.sem_inc(passed_pool, 1)

            def scatter(b_, par):
                pool.wait_ge(slot_maxed, value(b_, NSLOT, NSLOT))
                pool.sem_inc(passed_pool, 1)
                pool.wait_ge(turned, value(b_, NT, CREDIT - NT))
                pool.sem_inc(passed_pool, 1)
                for t in range(NT):
                    pool.indirect_dma_start(
                        agg_dram[par], bass.IndirectOffsetOnAxis(ap=perm[:, par, t:t + 1], axis=0),
                        agg[:, t, :], None, bounds_check=N - 1, oob_is_err=False,
                    ).then_inc(scattered[t // QT], 16)

            def first_slot_early(i, par):
                for s in h_stored:
                    pool.wait_ge(s, value(i, 16 * NQ, 16 * NQ))
                    pool.sem_inc(passed_pool, 1)
                pool.wait_ge(buf_b_zeroed, value(i, 1, 1))
                pool.sem_inc(passed_pool, 1)
                n = pool.value_load(n_tiles[0:1, par, S - 1:S])
                pairs = pool.value_load(n_tiles[0:1, par, S:S + 1])
                for t in range(2, NT):
                    with pool.If(pairs <= t // 2):
                        with pool.If(n > t):
                            gather(buf_b[:, 0, t - 2, :], par, idx[:, par, 0, t:t + 1], gathered_first)
                        pool.sem_inc(passed_pool, 1)

            def first_slot_late(i, par):
                pool.wait_ge(idx_ready, value(i, 1, 1))
                pool.sem_inc(passed_pool, 1)
                pool.wait_ge(buf_a_zeroed, value(i, 1, 1))
                pool.sem_inc(passed_pool, 1)
                n = pool.value_load(n_tiles[0:1, par, S - 1:S])
                pairs = pool.value_load(n_tiles[0:1, par, S:S + 1])
                with pool.If(n > 0):
                    gather(buf_a[:, RING_A - 1, 0, :], par, idx[:, par, 0, 0:1], gathered_first)
                with pool.If(n > 1):
                    gather(buf_a[:, RING_A - 1, 1, :], par, idx[:, par, 0, 1:2], gathered_first)
                with pool.If(pairs > 1):
                    for t in range(2, NT):
                        with pool.If(pairs > t // 2):
                            with pool.If(n > t):
                                gather(buf_b[:, 0, t - 2, :], par, idx[:, par, 0, t:t + 1], gathered_first)
                            pool.sem_inc(passed_pool, 1)
                    pool.sem_inc(passed_pool, 1)

            def one_slot(i, par, k):
                n = pool.value_load(n_tiles[0:1, par, S - 1 - k:S - k])
                r = (k - 1) % RING_A

                def one(t):
                    dst = buf_a[:, r, t, :] if t < 2 else buf_b[:, k % RING_B, t - 2, :]
                    if k == 2 and t == HALF:
                        pool.wait_ge(slot_maxed, value(i, NSLOT, 1))
                        pool.sem_inc(passed_pool, 1)
                    gather(dst, par, idx[:, par, k, t:t + 1], gathered_high if k == 1 and t >= HALF else gathered[r])

                if k == RING_A:
                    pool.wait_ge(slot_maxed, value(i, NSLOT, 1))
                    pool.sem_inc(passed_pool, 1)
                with pool.If(n > 0):
                    one(0)
                    with pool.If(n > 1):
                        one(1)
                    with pool.If(n > 2):
                        if k == 2:
                            pool.wait_ge(low_maxed, value(i, 1, 1))
                            pool.sem_inc(passed_pool, 1)
                        if k > 2:
                            pool.wait_ge(slot_maxed, value(i, NSLOT, max(k - RING_B, 1)))
                            pool.sem_inc(passed_pool, 1)
                        past_two(n, one)
                    pool.sem_inc(passed_pool, 1)

            def four_slots(i, par, g):
                k0 = SINGLE + 1 + 4 * g
                n = pool.value_load(n_tiles[0:1, par, S - 1 - k0:S - k0])

                def four(t):
                    for k in range(k0, k0 + 4):
                        gather(buf_a[:, (k - 1) % RING_A, t, :], par, idx[:, par, k, t:t + 1],
                               gathered_tail[g % 2][t])

                with pool.If(n > 0):
                    pool.wait_ge(slot_maxed, value(i, NSLOT, k0 + 3 - RING_A))
                    pool.sem_inc(passed_pool, 1)
                    four(0)
                    with pool.If(n > 1):
                        four(1)
                    with pool.If(n > 2):
                        for k in range(k0, k0 + 4):
                            if k - RING_B < k0:
                                pool.wait_ge(slot_maxed, value(i, NSLOT, min(k - RING_B, k0 - 1)))
                            else:
                                pool.wait_ge(rest_maxed, pool.snap(rest_done, min_val=0, max_val=60000) + (k - RING_B - k0 + 1))
                            pool.sem_inc(passed_pool, 1)
                            past_two(n, lambda t: gather(buf_b[:, k % RING_B, t - 2, :], par, idx[:, par, k, t:t + 1],
                                                         gathered[(k - 1) % RING_A]))
                        pool.reg_add(rest_done, rest_done, 4)
                    pool.sem_inc(passed_pool, 1)

            def iteration(i, par, with_next=True):
                other = 1 - par
                first_slot_late(i, par)
                for k in range(1, SINGLE + 1):
                    one_slot(i, par, k)
                four_slots(i, par, 0)
                if with_next:
                    heavy(i + 1, other)
                for g4 in range(1, NGRP):
                    four_slots(i, par, g4)
                if with_next:
                    first_slot_early(i + 1, other)
                scatter(i, par)

            rest_done = pool.alloc_register("rest_done")
            pool.reg_mov(rest_done, 0)
            heavy(0, 0)
            first_slot_early(0, 0)
            iteration(0, 0)
            with pool.Fori(0, B // 2 - 1) as pair:
                iteration(pair * 2 + 1, 1)
                iteration(pair * 2 + 2, 0)
            iteration(B - 1, 1, with_next=False)

        @block.scalar
        def _(act):
            a = nc.scalar
            act.wait_ge(const_dve, 10)
            act.wait_ge(const_landed, 64)

            def zero_a(i):
                if due(level := value(i, NSLOT, 0)):
                    act.wait_ge(slot_maxed, level)
                    act.sem_inc(passed_act, 1)
                a.activation(buf_a[:, :, :, :].rearrange("p r t c -> p (r t) c"),
                             zeros[:, :].unsqueeze(1).to_broadcast([P, RING_A * 2, C]),
                             ACT.Copy).then_inc(buf_a_zeroed, 1)

            def zero_b(i):
                if due(level := value(i, 1, 0)):
                    act.wait_ge(buf_b_free, level)
                    act.sem_inc(passed_act, 1)
                a.activation(buf_b[:, :, :, :].rearrange("p r t c -> p (r t) c"),
                             zeros[:, :].unsqueeze(1).to_broadcast([P, RING_B * (NT - 2), C]),
                             ACT.Copy).then_inc(buf_b_zeroed, 1)

            def sign_tile(nb, t):
                if t % QT == 0:
                    if due(level := value(nb, NQ, t // QT - 1)):
                        act.wait_ge(signs_used, level)
                        act.sem_inc(passed_act, 1)
                act.wait_ge(adj_landed[t % RING_ADJ],
                            value(nb, 16 * len(range(t % RING_ADJ, NT, RING_ADJ)), 16 * (t // RING_ADJ) + 16))
                a.activation(
                    signs[:, t // QT % 2, t % QT, :].rearrange("p (w j e) -> p w e j", j=8, e=4),
                    adj_in[:, t % RING_ADJ, :].rearrange("p (w e j) -> p w e j", e=4, j=8),
                    ACT.Sign).then_inc(signed, 1)

            def store_bits(nb):
                act.wait_ge(bits_packed, value(nb, NQ, NQ))
                act.sem_inc(passed_act, 1)
                if due(level := value(nb, 1, 0)):
                    act.wait_ge(idx_ready, level)
                    act.sem_inc(passed_act, 1)
                act.dma_start(bits_rows, bits[:, :, :]).then_inc(bits_stored, 16)

            def std_half(nb, half):
                t0, t1 = half * NT // 2, (half + 1) * NT // 2
                act.wait_ge(stats_ready, value(nb, 2, half + 1))
                a.activation(std[:, t0:t1], mean_var[:, t0:t1, 1], ACT.Sqrt, bias=eps[:, :]).then_inc(std_ready, 1)

            def norm(nb, par, half):
                t0, t1 = half * NT // 2, (half + 1) * NT // 2
                if due(level := value(nb, NSLOT, -NSLOT)):
                    act.wait_ge(slot_maxed, level)
                    act.sem_inc(passed_act, 1)
                act.wait_ge(norm_ready, value(nb, 2, half + 1))
                act.sem_inc(passed_act, 1)
                for pair_t in range(t0 // 2, t1 // 2):
                    if due(level := value(nb, 16 * NQ, 16 * (pair_t // 2))):
                        act.wait_ge(h_stored[pair_t % 2], level)
                        act.sem_inc(passed_act, 1)
                    for t in range(2 * pair_t, 2 * pair_t + 2):
                        a.activation(h_out[:, pair_t % 2, t % 2, :], xs[:, par, t, :], ACT.Relu,
                                     bias=shift[:, par, t:t + 1], scale=rstd[:, par, t:t + 1]).then_inc(h_written, 1)
                    act.wait_ge(h_written, value(nb, NT, 2 * pair_t + 2))
                    act.sem_inc(passed_act, 1)
                    act.dma_start(h_rows[par][:, 2 * pair_t:2 * pair_t + 2, :],
                                  h_out[:, pair_t % 2, :, :]).then_inc(h_stored[pair_t % 2], 16)

            def load_agg(b_, par, q):
                if q == 0:
                    for s in scattered:
                        act.wait_ge(s, value(b_, 16 * QT, 16 * QT))
                        act.sem_inc(passed_act, 1)
                act.wait_ge(y_added, value(b_, NQ, user_before(q, RING_AGG, NQ) + 1 + CREDIT))
                act.sem_inc(passed_act, 1)
                act.dma_start(agg_in[:, q % RING_AGG, :, :], agg_rows[par][:, q * QT:(q + 1) * QT, :]).then_inc(agg_landed[q], 16)

            def h_again(b_, par, t):
                act.wait_ge(turned, value(b_, NT, t - 1 + CREDIT))
                a.activation(h_tile[:, t % 2, :], xs[:, par, t, :], ACT.Relu, bias=shift[:, par, t:t + 1],
                             scale=rstd[:, par, t:t + 1]).then_inc(h_ready, 1)

            def join(b_, t):
                act.wait_ge(y_ready, value(b_, NT, t - 1 + CREDIT))
                act.wait_ge(turned, value(b_, NT, t + 1 + CREDIT))
                act.sem_inc(passed_act, 1)
                a.activation(joined_t[:, t % 2, :], turned_ps[t % 2][:, :], ACT.Copy).then_inc(joined, 1)

            def relu_y(b_, t):
                act.wait_ge(y_ready, value(b_, NT, t + 1 + CREDIT))
                a.activation(agg_in[:, t // QT % RING_AGG, t % QT, :], y_ps[t % 2][:, :], ACT.Relu).then_inc(y_copied, 1)

            def store_out(b_, par, q):
                act.wait_ge(y_added, value(b_, NQ, q + 1 + CREDIT))
                act.sem_inc(passed_act, 1)
                act.dma_start(out_rows[b_, :, q * QT:(q + 1) * QT, :],
                              xs[:, par, q * QT:(q + 1) * QT, :]).then_inc(out_stored[q], 16)

            def products(b_, par, sign_of):
                load_agg(b_, par, 0)
                load_agg(b_, par, 1)
                h_again(b_, par, 0)
                for t in range(NT):
                    if t % QT == 0 and 0 < t // QT < NQ - 1:
                        load_agg(b_, par, t // QT + 1)
                    if t + 1 < NT:
                        h_again(b_, par, t + 1)
                    join(b_, t)
                    if sign_of is not None and QT + t < NT:
                        sign_tile(sign_of, QT + t)
                    if t > 0:
                        relu_y(b_, t - 1)
                    if t % QT == QT - 1 and t > QT:
                        store_out(b_, par, t // QT - 1)
                relu_y(b_, NT - 1)

            def iteration(i, par, with_a=True, with_next=True, with_b=True, with_c=True):
                other = 1 - par
                with_next = with_a and with_next
                signs_of = i + 2 if with_next else None
                if with_b:
                    zero_a(i)
                if with_c and with_next:
                    for t in range(QT):
                        sign_tile(i + 2, t)
                if with_a:
                    store_bits(i + 1)
                if with_c:
                    products(i - 1, other, signs_of)
                if with_a:
                    std_half(i + 1, 0)
                if with_c:
                    store_out(i - 1, other, 3)
                if with_a:
                    norm(i + 1, other, 0)
                    std_half(i + 1, 1)
                    norm(i + 1, other, 1)
                first = 0
                if with_next and with_b and not with_c:
                    first = 2 * QT
                    for t in range(first):
                        sign_tile(i + 2, t)
                if with_a:
                    zero_b(i + 1)
                if with_next and not with_c:
                    for t in range(first, NT):
                        sign_tile(i + 2, t)

            act.sem_inc(joined, CREDIT)
            act.sem_inc(y_copied, CREDIT)
            for t in range(NT):
                sign_tile(0, t)
            iteration(-1, 1, with_b=False, with_c=False)
            iteration(0, 0, with_c=False)
            with act.Fori(0, B // 2 - 2) as pair:
                iteration(pair * 2 + 1, 1)
                iteration(pair * 2 + 2, 0)
            iteration(B - 3, 1)
            iteration(B - 2, 0, with_next=False)
            iteration(B - 1, 1, with_a=False)
            iteration(B, 0, with_a=False, with_b=False)

        @block.tensor
        def _(pe):
            pe.wait_ge(const_pool, 7)
            pe.wait_ge(const_dve, 10)
            pe.wait_ge(const_landed, 64)
            pe.wait_ge(bias_step, 8)

            def turn(b_, t):
                pe.wait_ge(joined, value(b_, NT, t - 1 + CREDIT))
                pe.wait_ge(h_ready, value(b_, NT, t + 1))
                pe.sem_inc(passed_pe, 1)
                if t % QT == 0:
                    pe.wait_ge(agg_landed[t // QT], value(b_, 16, 16))
                    pe.sem_inc(passed_pe, 1)
                for c in range(KC):
                    src = h_tile[:, t % 2, c * P:(c + 1) * P] if c < 2 else agg_in[:, t // QT % RING_AGG, t % QT, (c - 2) * P:(c - 1) * P]
                    last = nc.tensor.transpose(turned_ps[t % 2][:, c * P:(c + 1) * P], src, ident[:, :])
                last.then_inc(turned, 1)

            def multiply(b_, t):
                pe.wait_ge(y_copied, value(b_, NT, t - 1 + CREDIT))
                pe.wait_ge(joined, value(b_, NT, t + 1 + CREDIT))
                pe.sem_inc(passed_pe, 1)
                nc.tensor.matmul(y_ps[t % 2][:, :], ones_bf[0:3, :], b_parts[:, :], start=True, stop=False)
                for c in range(KC):
                    last = nc.tensor.matmul(y_ps[t % 2][:, :], joined_t[:, t % 2, c * P:(c + 1) * P], w_sb[:, c, :],
                                            start=False, stop=(c == KC - 1))
                last.then_inc(y_ready, 1)

            def products(b_, t0, t1):
                if t0 == 0:
                    turn(b_, 0)
                for t in range(t0, t1):
                    if t + 1 < NT:
                        turn(b_, t + 1)
                    multiply(b_, t)

            def histogram(nb):
                pe.wait_ge(onehot_ready, value(nb, 1, 1))
                flat = onehot[:, :, :].rearrange("p v t -> p (v t)")
                nc.tensor.matmul(before_ps[:, :], before[:, :], flat, start=True, stop=True)
                nc.tensor.matmul(total_ps[:, :], ones_bf[:, :], flat, start=True, stop=True).then_inc(hist_ready, 1)

            def carry(nb, s0, s1):
                for s in range(s0, s1):
                    pe.wait_ge(select_ready, value(nb, NT, s + 1))
                    for d in range(NT):
                        last = nc.tensor.matmul(
                            ranked_ps[:, d * COLS:(d + 1) * COLS], select[:, s % 2, d * P:(d + 1) * P],
                            carried[:, s, :], start=(s == 0 and d == 0), stop=(s == NT - 1), skip_group_check=True)
                    last.then_inc(carried_step, 1)

            pe.sem_inc(turned, CREDIT)
            pe.sem_inc(y_ready, CREDIT)
            def iteration(i, with_a=True):
                if with_a:
                    histogram(i + 1)
                products(i - 1, 0, 10)
                if with_a:
                    carry(i + 1, 0, 8)
                products(i - 1, 10, 16)
                if with_a:
                    carry(i + 1, 8, 16)

            histogram(0)
            carry(0, 0, NT)
            histogram(1)
            carry(1, 0, NT)
            with pe.Fori(0, B // 2 - 1) as pair:
                iteration(pair * 2 + 1)
                iteration(pair * 2 + 2)
            iteration(B - 1, with_a=False)
            iteration(B, with_a=False)

        @block.vector
        def _(dve):
            v = nc.vector
            total_first = dve.alloc_register("total_first")
            total_high = dve.alloc_register("total_high")
            totals = [dve.alloc_register(f"total{i}") for i in range(RING_A)]
            totals_tail = [[dve.alloc_register(f"total_tail{i}_{t}") for t in range(2)] for i in range(2)]
            rest_done = dve.alloc_register("rest_done")
            heavy_total = dve.alloc_register("heavy_total")
            heavy_done = dve.alloc_register("heavy_done")
            for r in (total_first, total_high, *totals, *totals_tail[0], *totals_tail[1], rest_done, heavy_total, heavy_done):
                dve.reg_mov(r, 0)

            def read(r):
                return dve.snap(r, min_val=0, max_val=60000)

            v.memset(zeros[:, :], 0.0)
            v.memset(ones_f[:, :], 1.0)
            v.memset(ones_bf[:, :], 1.0)
            v.memset(eps[:, :], EPS)
            for i in range(GROUP):
                v.memset(bit_of[:, i:i + 1], 1 << i)
                v.memset(pick[:, i:i + 1], (1 << (7 + i)) | 127)
                v.memset(bit_late[:, i:i + 1], float(GROUP - i))
            for t in range(NT):
                ins = v.memset(tile_no[:, t:t + 1], float(t))
            ins.then_inc(const_dve, 1)
            dve.wait_ge(const_pool, 7)
            v.tensor_copy(group_no[:, :], iota_i[:, :]).then_inc(const_dve, 1)
            dve.wait_ge(const_dve, 2)
            v.tensor_scalar(group_late[:, :], group_no[:, :], -65536.0, 65536.0 * (NG - 1), ALU.mult,
                            ALU.add).then_inc(const_dve, 1)
            v.tensor_scalar(counts_down[:, :], group_no[:, 0:NV], -1.0, float(S), ALU.mult,
                            ALU.add).then_inc(const_dve, 1)
            for t in range(NT):
                ins = v.tensor_copy(carried[:, t, 2 * LIGHT:2 * LIGHT + 1], row_in_tile[:, :])
            ins.then_inc(const_dve, 1)
            v.tensor_copy(carried[:, :, 2 * LIGHT + 1], tile_no[:, :]).then_inc(const_dve, 5)
            dve.sem_inc(y_added, CREDIT)
            dve.wait_ge(const_landed, 64)
            v.tensor_copy(b_part[:, 0, :], b_sb[:, :]).then_inc(bias_step, 1)
            dve.wait_ge(bias_step, 1)
            v.tensor_tensor(b_sb[:, :], b_sb[:, :], b_part[:, 0, :], ALU.subtract).then_inc(bias_step, 1)
            dve.wait_ge(bias_step, 2)
            v.tensor_copy(b_part[:, 1, :], b_sb[:, :]).then_inc(bias_step, 1)
            dve.wait_ge(bias_step, 3)
            v.tensor_tensor(b_sb[:, :], b_sb[:, :], b_part[:, 1, :], ALU.subtract).then_inc(bias_step, 1)
            dve.wait_ge(bias_step, 4)
            v.tensor_copy(b_part[:, 2, :], b_sb[:, :]).then_inc(bias_step, 1)
            dve.wait_ge(bias_step, 5)
            v.tensor_scalar(b_sum[:, :], b_part[:, 0, :], ident[0:3, 0:1], None, ALU.mult).then_inc(bias_step, 1)
            dve.wait_ge(bias_step, 6)
            v.scalar_tensor_tensor(b_sum[:, :], b_part[:, 1, :], ident[0:3, 1:2], b_sum[:, :], ALU.mult,
                                   ALU.add).then_inc(bias_step, 1)
            dve.wait_ge(bias_step, 7)
            v.scalar_tensor_tensor(b_parts[:, :], b_part[:, 2, :], ident[0:3, 2:3], b_sum[:, :], ALU.mult,
                                   ALU.add).then_inc(bias_step, 1)

            def load_counts(counts, par, ks):
                for k in ks:
                    counts[k] = dve.value_load(n_tiles[0:1, par, S - 1 - k:S - k], min_val=0, max_val=NT)

            PACK = 7

            def pack_quad(nb, q, counts=None, par=0, ks=((), ())):
                def step(n):
                    return value(nb, PACK * NQ, PACK * q + n)
                s = signs[:, q % 2, :, :].rearrange("p t n -> p (t n)").bitcast(U32)
                dve.wait_ge(signed, value(nb, NT, (q + 1) * QT))
                v.tensor_scalar(s, s, 0x01010101, None, ALU.bitwise_and).then_inc(pack_step, 1)
                load_counts(counts, par, ks[0])
                if due(level := value(nb, NQ, q)):
                    dve.wait_ge(found_ready, level)
                    dve.sem_inc(passed_dve, 1)
                dve.wait_ge(pack_step, step(1))
                two = s.rearrange("p (n two) -> p n two", two=2)
                v.scalar_tensor_tensor(half1, two[:, :, 1], 1, two[:, :, 0], ALU.logical_shift_left,
                                       ALU.bitwise_or).then_inc(pack_step, 1)
                load_counts(counts, par, ks[1])
                dve.wait_ge(pack_step, step(2))
                dve.sem_inc(passed_dve, 1)
                dve.sem_inc(signs_used, 1)
                two = half1.rearrange("p (n two) -> p n two", two=2)
                v.scalar_tensor_tensor(half2, two[:, :, 1], 2, two[:, :, 0], ALU.logical_shift_left,
                                       ALU.bitwise_or).then_inc(pack_step, 1)
                if q == 0:
                    if due(level := value(nb, 16, 0)):
                        dve.wait_ge(bits_stored, level)
                dve.wait_ge(pack_step, step(3))
                two = half2.rearrange("p (n two) -> p n two", two=2)
                quad = bits[:, q * QT:(q + 1) * QT, :]
                v.scalar_tensor_tensor(quad.rearrange("p t w -> p (t w)"), two[:, :, 1], 4, two[:, :, 0],
                                       ALU.logical_shift_left, ALU.bitwise_or).then_inc(pack_step, 1)
                dve.wait_ge(pack_step, step(4))
                dve.sem_inc(passed_dve, 1)
                dve.sem_inc(bits_packed, 1)
                v.scalar_tensor_tensor(keys[:, :, :], quad.bitcast(U16), 128.0,
                                       group_no[:, :].unsqueeze(1).to_broadcast([P, QT, NG]),
                                       ALU.mult, ALU.add).then_inc(pack_step, 1)
                dve.wait_ge(pack_step, step(5))
                dve.sem_inc(passed_dve, 1)
                for t in range(QT):
                    ins = v.max(top_groups[:, t, :], keys[:, t, :])
                ins.then_inc(pack_step, 1)
                dve.wait_ge(pack_step, step(6))
                v.tensor_tensor(cand[:, :, :, :].rearrange("p t g i -> p (t g) i"),
                                top_groups[:, :, :].rearrange("p t g -> p (t g)").unsqueeze(2).to_broadcast([P, QT * 8, GROUP]),
                                pick[:, :].unsqueeze(1).to_broadcast([P, QT * 8, GROUP]),
                                ALU.bitwise_and).then_inc(pack_step, 1)
                dve.wait_ge(pack_step, step(7))
                dve.sem_inc(passed_dve, 1)
                for t in range(QT):
                    ins = v.max(found[:, q * QT + t, :], cand[:, t, :, :].rearrange("p g i -> p (g i)"))
                ins.then_inc(found_ready, 1)

            NORM = 6

            def norm_stats(nb, par, half):
                t0, t1 = half * NT // 2, (half + 1) * NT // 2
                for q in range(2 * half, 2 * half + 2):
                    dve.wait_ge(x_landed[q], value(nb, 16, 16))
                    dve.sem_inc(passed_dve, 1)
                for t in range(t0, t1):
                    ins = v.bn_stats(stats[:, t, :], xs[:, par, t, :])
                ins.then_inc(norm_step, 1)
                if due(level := value(nb, 2, half - 1)):
                    dve.wait_ge(std_ready, level)
                    dve.sem_inc(passed_dve, 1)
                dve.wait_ge(norm_step, value(nb, NORM, 3 * half + 1))
                dve.sem_inc(passed_dve, 1)
                for t in range(t0, t1):
                    ins = v.bn_aggr(mean_var[:, t, :], stats[:, t, :])
                ins.then_inc(stats_ready, 1)

            def norm_scale(nb, par, half):
                t0, t1 = half * NT // 2, (half + 1) * NT // 2
                if due(level := value(nb, NT, t1 - 2 * NT)):
                    dve.wait_ge(h_ready, level)
                    dve.sem_inc(passed_dve, 1)
                dve.wait_ge(std_ready, value(nb, 2, half + 1))
                v.reciprocal(rstd[:, par, t0:t1], std[:, t0:t1]).then_inc(norm_step, 1)
                dve.wait_ge(norm_step, value(nb, NORM, 3 * half + 2))
                v.scalar_tensor_tensor(shift[:, par, t0:t1], mean_var[:, t0:t1, 0], -1.0, rstd[:, par, t0:t1], ALU.mult,
                                       ALU.mult).then_inc(norm_step, 1)
                dve.wait_ge(norm_step, value(nb, NORM, 3 * half + 3))
                dve.sem_inc(norm_ready, 1)

            RANK = 36

            def count_rows(nb, steps):
                f2 = found[:, :, :].rearrange("p t k -> p (t k)")
                dve.wait_ge(found_ready, value(nb, NQ, NQ))
                v.tensor_copy(found_f[:, :], f2).then_inc(found_step, steps.up())
                dve.wait_ge(found_step, steps.now)
                v.tensor_scalar(found_f[:, :].bitcast(I32), found_f[:, :].bitcast(I32), 23, None,
                                     ALU.logical_shift_right).then_inc(found_step, steps.up())
                v.tensor_scalar(f2, f2, 127, None, ALU.bitwise_and).then_inc(found_step, steps.up())
                dve.wait_ge(found_step, steps.now)
                dve.sem_inc(passed_dve, 1)
                if due(level := value(nb, NT, 0)):
                    dve.wait_ge(carried_step, level)
                v.tensor_copy(carried[:, :, 0:LIGHT], found[:, :, :]).then_inc(found_step, steps.up())
                v.tensor_scalar(carried[:, :, LIGHT:2 * LIGHT],
                                     found_f[:, :].bitcast(I32).rearrange("p (t k) -> p t k", k=8),
                                     -133.0, 0.0, ALU.add, ALU.max).then_inc(found_step, steps.up())

                half = bits[:, :, :].rearrange("p t w -> p (t w)").bitcast(U16)
                pa, pb = pop_a, pop_b
                v.tensor_scalar(pa, half, 1, 0x5555, ALU.logical_shift_right, ALU.bitwise_and).then_inc(found_step, steps.up())
                dve.wait_ge(found_step, steps.now)
                v.tensor_tensor(pb, half, pa, ALU.subtract).then_inc(found_step, steps.up())
                dve.wait_ge(found_step, steps.now)
                v.tensor_scalar(pa, pb, 2, 0x3333, ALU.logical_shift_right, ALU.bitwise_and).then_inc(found_step, steps.up())
                dve.wait_ge(found_step, steps.now)
                v.tensor_scalar(pb, pb, 0x3333, None, ALU.bitwise_and).then_inc(found_step, steps.up())
                dve.wait_ge(found_step, steps.now)
                v.tensor_tensor(pa, pa, pb, ALU.add).then_inc(found_step, steps.up())
                pa2, pb2 = pa[:, 0:NT * NG // 2], pb[:, 0:NT * NG // 2]
                both = pa.rearrange("p (t h n) -> p t h n", t=NT, h=2)
                dve.wait_ge(found_step, steps.now)
                v.tensor_tensor(pb2.rearrange("p (t n) -> p t n", t=NT), both[:, :, 0, :], both[:, :, 1, :],
                                ALU.add).then_inc(found_step, steps.up())
                dve.wait_ge(found_step, steps.now)
                v.tensor_scalar(pa2, pb2, 4, 0x0F0F, ALU.logical_shift_right, ALU.bitwise_and).then_inc(found_step, steps.up())
                v.tensor_scalar(pb2, pb2, 0x0F0F, None, ALU.bitwise_and).then_inc(found_step, steps.up())
                dve.wait_ge(found_step, steps.now)
                v.tensor_tensor(pa2, pa2, pb2, ALU.add).then_inc(found_step, steps.up())
                dve.wait_ge(found_step, steps.now)
                n = NG // 2
                src, dst = pop_a, pop_b
                while n > 8:
                    sv = src[:, 0:NT * n].rearrange("p (t h n) -> p t h n", t=NT, h=2)
                    dv = dst[:, 0:NT * n // 2].rearrange("p (t n) -> p t n", t=NT)
                    v.tensor_tensor(dv, sv[:, :, 0, :], sv[:, :, 1, :], ALU.add).then_inc(found_step, steps.up())
                    dve.wait_ge(found_step, steps.now)
                    src, dst, n = dst, src, n // 2
                v.tensor_reduce(count[:, :], src[:, 0:NT * n].bitcast(U8).rearrange("p (t n) -> p t n", t=NT),
                                     AX_X, ALU.add).then_inc(found_step, steps.up())
                dve.wait_ge(found_step, steps.now)
                v.tensor_scalar(count[:, :], count[:, :], float(S), None, ALU.min).then_inc(found_step, steps.up())
                dve.wait_ge(found_step, steps.now)
                dve.sem_inc(passed_dve, 1)
                if due(level := value(nb, 1, 0)):
                    dve.wait_ge(hist_ready, level)
                v.tensor_tensor(onehot[:, :, :], count[:, :].unsqueeze(1).to_broadcast([P, NV, NT]),
                                counts_down[:, :].unsqueeze(2).to_broadcast([P, NV, NT]),
                                ALU.is_equal).then_inc(onehot_ready, 1)

            def rank_rows(nb, steps):
                dve.wait_ge(hist_ready, value(nb, 1, 1))
                v.tensor_tensor_scan(cum[:, :], ones_f[:, :], total_ps[:, :], 0.0, ALU.mult, ALU.add).then_inc(found_step, steps.up())
                dve.wait_ge(found_step, steps.now)
                v.tensor_tensor(spot[:, :], cum[:, :], total_ps[:, :], ALU.subtract).then_inc(found_step, steps.up())
                dve.wait_ge(found_step, steps.now)
                v.tensor_tensor(spot[:, :], spot[:, :], before_ps[:, :], ALU.add).then_inc(found_step, steps.up())
                dve.wait_ge(found_step, steps.now)
                v.tensor_tensor(spot[:, :], spot[:, :], onehot[:, :, :].rearrange("p v t -> p (v t)"), ALU.mult).then_inc(found_step, steps.up())
                dve.wait_ge(found_step, steps.now)
                v.tensor_reduce(rank[:, :], spot[:, :].rearrange("p (v t) -> p t v", v=NV), AX_X, ALU.add).then_inc(found_step, steps.up())
                dve.wait_ge(found_step, steps.now)
                dve.sem_inc(passed_dve, 1)

            def select_rows(nb, s0, s1):
                for s in range(s0, s1):
                    if due(level := value(nb, NT, s - 1)):
                        dve.wait_ge(carried_step, level)
                    v.tensor_scalar(select[:, s % 2, :], position[:, :], rank[:, s:s + 1], None,
                                    ALU.is_equal).then_inc(select_ready, 1)

            def index_rows(nb, par, steps):
                for s in scattered:
                    if due(level := value(nb, 16 * QT, -16 * QT)):
                        dve.wait_ge(s, level)
                more_than = cum[:, :].rearrange("p (v t) -> p v t", v=NV)
                v.tensor_scalar(tiles_f[:, 0:S], more_than[:, 0:S, NT - 1], float(P - 1), None,
                                ALU.add).then_inc(found_step, steps.up())
                v.tensor_scalar(tiles_f[:, S:S + 1], more_than[:, S - 1 - LIGHT:S - LIGHT, NT - 1], float(2 * P - 1), None,
                                ALU.add).then_inc(found_step, steps.up())
                dve.wait_ge(found_step, steps.now)
                v.tensor_scalar(n_tiles[:, par, 0:S], tiles_f[:, 0:S], 7, None,
                                ALU.logical_shift_right).then_inc(found_step, steps.up())
                v.tensor_scalar(n_tiles[:, par, S:S + 1], tiles_f[:, S:S + 1], 8, None,
                                ALU.logical_shift_right).then_inc(found_step, steps.up())
                dve.wait_ge(found_step, steps.now - 1)
                v.tensor_scalar(n_past_two[:, par, :], n_tiles[:, par, 0:S], -2.0, 0.0, ALU.add,
                                ALU.max).then_inc(found_step, steps.up())
                v.tensor_scalar(n_high[:, par, :], n_tiles[:, par, S - 2:S - 1], -float(HALF), 0.0, ALU.add,
                                ALU.max).then_inc(found_step, steps.up())
                dve.wait_ge(carried_step, value(nb, NT, NT))
                v.tensor_copy(ranked[:, :, :].rearrange("p t c -> p (t c)"), ranked_ps[:, :]).then_inc(found_step, steps.up())
                dve.wait_ge(found_step, steps.now)
                dve.sem_inc(passed_dve, 1)
                group, bit1 = ranked[:, :, 0:LIGHT], ranked[:, :, LIGHT:2 * LIGHT]
                so = slot_of[:, :].rearrange("p (t k) -> p t k", k=8)
                no = no_slot[:, :].rearrange("p (t k) -> p t k", k=8)
                v.scalar_tensor_tensor(so, group, float(GROUP), bit1, ALU.mult, ALU.add).then_inc(found_step, steps.up())
                v.tensor_scalar(no, bit1, 0.0, float(SKIP), ALU.is_equal, ALU.mult).then_inc(found_step, steps.up())
                v.scalar_tensor_tensor(row_of[:, :], ranked[:, :, 2 * LIGHT + 1], float(P),
                                            ranked[:, :, 2 * LIGHT], ALU.mult, ALU.add).then_inc(found_step, steps.up())
                dve.wait_ge(found_step, steps.now)
                v.scalar_tensor_tensor(idx[:, par, 0:LIGHT, :].rearrange("p k t -> p t k"), so, -1.0, no,
                                            ALU.add, ALU.add).then_inc(found_step, steps.up())
                v.tensor_copy(perm[:, par, :], row_of[:, :]).then_inc(found_step, steps.up())
                dve.wait_ge(found_step, steps.now)
                dve.sem_inc(passed_dve, 1)
                dve.sem_inc(ranked_ready, 1)
                assert steps.n == RANK, steps.n

            HEAVY = 37

            def heavy_pair(par, d):
                steps = Steps(read(heavy_done))
                half = heavy_bits[:, bass.ds(d * 2, 2), :].rearrange("p t w -> p (t w)").bitcast(U16)
                key = heavy_key[:, :, :].rearrange("p t g -> p (t g)")
                late = group_late[:, :].unsqueeze(1).to_broadcast([P, 2, NG])
                v.scalar_tensor_tensor(heavy_key[:, :, :], half.rearrange("p (t g) -> p t g", t=2), 0.0, late, ALU.is_gt,
                                       ALU.mult).then_inc(heavy_step, steps.up())
                dve.wait_ge(heavy_step, steps.now)
                v.tensor_tensor(key, key, half, ALU.add).then_inc(heavy_step, steps.up())
                dve.wait_ge(heavy_step, steps.now)
                dve.sem_inc(passed_dve, 1)
                for r in range(4):
                    eights = [heavy_groups[:, t, 8 * r:8 * r + 8] for t in range(2)]
                    for t in range(2):
                        if r:
                            dve.wait_ge(heavy_step, steps.now - 1)
                            dve.sem_inc(passed_dve, 1)
                        v.max(eights[t], heavy_key[:, t, :]).then_inc(heavy_step, steps.up())
                    if r < 3:
                        for t in range(2):
                            dve.wait_ge(heavy_step, steps.now - 1)
                            dve.sem_inc(passed_dve, 1)
                            v.match_replace(heavy_key[:, t, :], eights[t], heavy_key[:, t, :],
                                            0.0).then_inc(heavy_step, steps.up())
                dve.wait_ge(heavy_step, steps.now)
                v.tensor_copy(heavy_gi[:, :].rearrange("p (t g) -> p t g", t=2), heavy_groups[:, :, 0:HG]).then_inc(heavy_step, steps.up())
                dve.wait_ge(heavy_step, steps.now)
                v.tensor_scalar(heavy_gp[:, :], heavy_gi[:, :], 16, 4, ALU.logical_shift_right,
                                ALU.logical_shift_left).then_inc(heavy_step, steps.up())
                v.tensor_tensor(heavy_bit[:, :, :], heavy_gi[:, :].unsqueeze(2).to_broadcast([P, 2 * HG, GROUP]),
                                bit_of[:, :].unsqueeze(1).to_broadcast([P, 2 * HG, GROUP]),
                                ALU.bitwise_and).then_inc(heavy_step, steps.up())
                dve.wait_ge(heavy_step, steps.now)
                v.tensor_tensor(heavy_pos[:, :, :], heavy_gp[:, :].unsqueeze(2).to_broadcast([P, 2 * HG, GROUP]),
                                bit_late[:, :].unsqueeze(1).to_broadcast([P, 2 * HG, GROUP]),
                                ALU.add).then_inc(heavy_step, steps.up())
                dve.wait_ge(heavy_step, steps.now)
                pos = heavy_pos[:, :, :].rearrange("p g i -> p (g i)")
                v.scalar_tensor_tensor(pos, heavy_bit[:, :, :].rearrange("p g i -> p (g i)"), 0.0, pos, ALU.is_gt,
                                       ALU.mult).then_inc(heavy_step, steps.up())
                dve.wait_ge(heavy_step, steps.now)
                dve.sem_inc(passed_dve, 1)
                of_tile = [pos[:, t * HG * GROUP:(t + 1) * HG * GROUP] for t in range(2)]
                for r in range(4):
                    eights = [heavy_cols[:, t, 8 * r:8 * r + 8] for t in range(2)]
                    for t in range(2):
                        if r:
                            dve.wait_ge(heavy_step, steps.now - 1)
                            dve.sem_inc(passed_dve, 1)
                        v.max(eights[t], of_tile[t]).then_inc(heavy_step, steps.up())
                    if r < 3:
                        for t in range(2):
                            dve.wait_ge(heavy_step, steps.now - 1)
                            dve.sem_inc(passed_dve, 1)
                            v.match_replace(of_tile[t], eights[t], of_tile[t], 0.0).then_inc(heavy_step, steps.up())
                dve.wait_ge(heavy_step, steps.now)
                v.tensor_scalar(heavy_none[:, :, :], heavy_cols[:, :, :], 0.0, float(SKIP), ALU.is_equal,
                                ALU.mult).then_inc(heavy_step, steps.up())
                dve.wait_ge(heavy_step, steps.now)
                v.scalar_tensor_tensor(idx[:, par, :, bass.ds(d * 2, 2)].rearrange("p k t -> p t k"),
                                       heavy_none[:, :, 0:S], float(N), heavy_cols[:, :, 0:S], ALU.add,
                                       ALU.subtract).then_inc(heavy_step, steps.up())
                assert steps.n == HEAVY, steps.n
                dve.reg_add(heavy_done, heavy_done, HEAVY)
                dve.wait_ge(heavy_step, read(heavy_done))
                dve.sem_inc(passed_dve, 1)

            def heavy_rows(i, par):
                n = dve.value_load(n_tiles[0:1, par, S:S + 1], min_val=0, max_val=NT // 2)
                dve.reg_add(heavy_total, heavy_total, n * 32)
                with dve.If(n > 0):
                    dve.wait_ge(heavy_landed, read(heavy_total))
                    dve.sem_inc(passed_dve, 1)
                    with dve.Fori(0, n) as d:
                        heavy_pair(par, d)
                    dve.sem_inc(passed_dve, 1)
                dve.sem_inc(idx_ready, 1)

            def maxed(lo, hi, k):
                src = buf_a[:, (k - 1) % RING_A, lo:hi, :] if hi <= 2 else buf_b[:, k % RING_B, lo - 2:hi - 2, :]
                dst = agg[:, lo:hi, :]
                return v.tensor_tensor(dst, dst, src, ALU.max)

            def first_two_slots(i, par, counts):
                n0, n1 = counts[0], counts[1]
                dve.reg_add(total_first, total_first, n0 * 16)
                with dve.If(n1 > HALF):
                    dve.reg_add(totals[0], totals[0], HALF * 16)
                    n_more = dve.value_load(n_high[0:1, par, :], min_val=0, max_val=NT)
                    dve.reg_add(total_high, total_high, n_more * 16)
                with dve.If(n1 <= HALF):
                    dve.reg_add(totals[0], totals[0], n1 * 16)
                for s in scattered:
                    if due(level := value(i, 16 * QT, 0)):
                        dve.wait_ge(s, level)
                        dve.sem_inc(passed_dve, 1)
                dve.wait_ge(buf_a_zeroed, value(i, 1, 1))
                dve.sem_inc(passed_dve, 1)
                dve.wait_ge(buf_b_zeroed, value(i, 1, 1))
                dve.sem_inc(passed_dve, 1)
                with dve.If(n0 > 0):
                    dve.wait_ge(gathered_first, read(total_first))
                    dve.sem_inc(passed_dve, 1)
                with dve.If(n1 > 0):
                    dve.wait_ge(gathered[0], read(totals[0]))
                    dve.sem_inc(passed_dve, 1)
                v.tensor_tensor(agg[:, 2:HALF, :], buf_b[:, 0, 0:HALF - 2, :], buf_b[:, 1, 0:HALF - 2, :],
                                ALU.max).then_inc(low_maxed, 1)
                v.tensor_tensor(agg[:, 0:2, :], buf_a[:, RING_A - 1, :, :], buf_a[:, 0, :, :], ALU.max)
                with dve.If(n1 > HALF):
                    dve.wait_ge(gathered_high, read(total_high))
                    dve.sem_inc(passed_dve, 1)
                v.tensor_tensor(agg[:, HALF:NT, :], buf_b[:, 0, HALF - 2:, :], buf_b[:, 1, HALF - 2:, :],
                                ALU.max).then_inc(slot_maxed, 1)

            def slot(i, counts, k):
                n = counts[k]
                total = totals[(k - 1) % RING_A]
                dve.reg_add(total, total, n * 16)
                if due(level := value(i, NSLOT, k - 1)):
                    dve.wait_ge(slot_maxed, level)
                    dve.sem_inc(passed_dve, 1)
                with dve.If(n > 0):
                    dve.wait_ge(gathered[(k - 1) % RING_A], read(total))
                    dve.sem_inc(passed_dve, 1)
                    with dve.If(n > 1):
                        with dve.If(n > 2):
                            with dve.If(n > 4):
                                with dve.If(n > 8):
                                    maxed(8, NT, k)
                                maxed(4, 8, k)
                            maxed(2, 4, k)
                        maxed(1, 2, k)
                    dve.sem_inc(passed_dve, 1)
                maxed(0, 1, k).then_inc(slot_maxed, 1)

            def free_buf_b(i, counts, now):
                n = counts[SINGLE + 1]
                dve.wait_ge(slot_maxed, value(i, NSLOT, now))
                dve.sem_inc(passed_dve, 1)
                with dve.If(n <= 2 if now == SINGLE else n > 2):
                    dve.sem_inc(buf_b_free, 1)

            def rest_of_four(n, par, k0):
                r = (k0 - 1) % RING_A
                n_rest = dve.value_load(n_past_two[0:1, par, S - 1 - k0:S - k0], min_val=0, max_val=NT)
                for j in range(4):
                    dve.reg_add(totals[r + j], totals[r + j], n_rest * 16)
                    dve.wait_ge(gathered[r + j], read(totals[r + j]))
                    dve.sem_inc(passed_dve, 1)
                    with dve.If(n > 4):
                        with dve.If(n > 8):
                            maxed(8, NT, k0 + j)
                        maxed(4, 8, k0 + j)
                    maxed(2, 4, k0 + j).then_inc(rest_maxed, 1)
                    dve.reg_add(rest_done, rest_done, 1)
                    dve.wait_ge(rest_maxed, read(rest_done))
                    dve.sem_inc(passed_dve, 1)

            def fold_four(i, g4, tiles):
                k0 = SINGLE + 1 + 4 * g4
                r = (k0 - 1) % RING_A
                pair = buf_a[:, r:r + 2, 0:tiles, :]
                v.tensor_tensor(pair, pair, buf_a[:, r + 2:r + 4, 0:tiles, :], ALU.max).then_inc(group_step, 1)
                dve.wait_ge(group_step, value(i, 2 * NGRP, 2 * g4 + 1))
                maxed(0, tiles, k0).then_inc(group_step, 1)
                dve.wait_ge(group_step, value(i, 2 * NGRP, 2 * g4 + 2))
                maxed(0, tiles, k0 + 1).then_inc(slot_maxed, 4)

            def four_slots(i, par, counts, g4):
                k0 = SINGLE + 1 + 4 * g4
                n = counts[k0]
                tail, total = gathered_tail[g4 % 2], totals_tail[g4 % 2]
                dve.wait_ge(slot_maxed, value(i, NSLOT, k0 - 1))
                dve.sem_inc(passed_dve, 1)
                with dve.If(n > 1):
                    with dve.If(n > 2):
                        rest_of_four(n, par, k0)
                    for t in range(2):
                        dve.reg_add(total[t], total[t], 4 * 16)
                        dve.wait_ge(tail[t], read(total[t]))
                        dve.sem_inc(passed_dve, 1)
                    fold_four(i, g4, 2)
                with dve.If(n <= 1):
                    with dve.If(n > 0):
                        dve.reg_add(total[0], total[0], 4 * 16)
                        dve.wait_ge(tail[0], read(total[0]))
                        dve.sem_inc(passed_dve, 1)
                    fold_four(i, g4, 1)

            def add_x(b_, par, q):
                dve.wait_ge(y_copied, value(b_, NT, (q + 1) * QT + CREDIT))
                quad = xs[:, par, q * QT:(q + 1) * QT, :]
                v.tensor_tensor(quad, quad, agg_in[:, q % RING_AGG, :, :], ALU.add).then_inc(y_added, 1)

            def iteration(i, par, with_a=True, with_next=True, with_b=True, with_c=True):
                nb, other = i + 1, 1 - par
                with_next = with_a and with_next
                steps = Steps(nb * RANK)
                counts = {}
                early, late = (((0, 1), (2, 3)), ((4, 5), (6, 7))) if with_b else (((), ()), ((), ()))
                if with_a:
                    pack_quad(nb, 2, counts, par, early)
                    pack_quad(nb, 3, counts, par, late)
                if with_a and not with_c:
                    norm_stats(nb, other, 0)
                    norm_scale(nb, other, 0)
                    norm_stats(nb, other, 1)
                    norm_scale(nb, other, 1)
                if with_b and not with_a:
                    load_counts(counts, par, range(SINGLE))
                if with_b and not (with_next and with_c):
                    load_counts(counts, par, (8, 9, 13, 17, 21))
                if with_a:
                    count_rows(nb, steps)
                    rank_rows(nb, steps)
                if with_next and with_c:
                    pack_quad(nb + 1, 0, counts, par, ((8, 9, 13), (17, 21)))
                if with_b:
                    first_two_slots(i, par, counts)
                if with_c:
                    add_x(i - 1, other, 0)
                if with_next and with_c:
                    pack_quad(nb + 1, 1)
                if with_c:
                    add_x(i - 1, other, 1)
                if with_a:
                    select_rows(nb, 0, 8)
                if with_b:
                    slot(i, counts, 2)
                    slot(i, counts, 3)
                if with_c:
                    add_x(i - 1, other, 2)
                if with_b:
                    slot(i, counts, 4)
                if with_a and with_c:
                    norm_stats(nb, other, 0)
                if with_c:
                    add_x(i - 1, other, 3)
                if with_b:
                    slot(i, counts, 5)
                if with_a:
                    select_rows(nb, 8, 12)
                if with_b:
                    slot(i, counts, 6)
                if with_a:
                    select_rows(nb, 12, 16)
                if with_b:
                    slot(i, counts, 7)
                if with_a:
                    index_rows(nb, other, steps)
                if with_a and with_c:
                    norm_scale(nb, other, 0)
                if with_b:
                    slot(i, counts, 8)
                    free_buf_b(i, counts, SINGLE)
                if with_a and with_c:
                    norm_stats(nb, other, 1)
                if with_b:
                    four_slots(i, par, counts, 0)
                if with_a and with_c:
                    norm_scale(nb, other, 1)
                if with_next and not with_c:
                    pack_quad(nb + 1, 0)
                    pack_quad(nb + 1, 1)
                if with_b:
                    four_slots(i, par, counts, 1)
                if with_a:
                    heavy_rows(nb, other)
                if with_b:
                    four_slots(i, par, counts, 2)
                    four_slots(i, par, counts, 3)
                    free_buf_b(i, counts, NSLOT)

            pack_quad(0, 0)
            pack_quad(0, 1)
            iteration(-1, 1, with_b=False, with_c=False)
            iteration(0, 0, with_c=False)
            with dve.Fori(0, B // 2 - 2) as pair:
                iteration(pair * 2 + 1, 1)
                iteration(pair * 2 + 2, 0)
            iteration(B - 3, 1)
            iteration(B - 2, 0, with_next=False)
            iteration(B - 1, 1, with_a=False)
            iteration(B, 0, with_a=False, with_b=False)


_INS = ["x", "adj", "L0_gnn_W", "L0_gnn_b"]


def kernel(**inputs):
    import numpy as _np
    import concourse.bacc as _bacc
    from concourse import mybir as _mybir
    from concourse.bass_utils import run_bass_kernel_spmd as _run

    nc = _bacc.Bacc("TRN2", target_bir_lowering=False, num_devices=1)
    arrays, args = {}, []
    for name in _INS:
        a = _np.ascontiguousarray(inputs[name])
        arrays[f"in_{name}_dram"] = a
        args.append(nc.dram_tensor(f"in_{name}_dram", a.shape, _mybir.dt.from_np(a.dtype), kind="ExternalInput").ap())
    shape = tuple(inputs["x"].shape)
    args.append(nc.dram_tensor("out_dram", shape, _mybir.dt.float32, kind="ExternalOutput").ap())
    build(nc, *args)
    r = _run(nc, [arrays], core_ids=[0])
    return r.results[0]["out_dram"]
```
